# Optimizing a Trainium2 kernel written in Bass

```python
import numpy as np
import jax
import jax.numpy as jnp

def _softmax(x, axis=-1):
    return jax.nn.softmax(x, axis=axis)

def _gelu(x):
    return jax.nn.gelu(x, approximate=True)

def _silu(x):
    return jax.nn.silu(x)

def _sigmoid(x):
    return jax.nn.sigmoid(x)

def _layernorm(x, axis=-1, eps=1e-05):
    m = jnp.mean(x, axis=axis, keepdims=True)
    v = jnp.var(x, axis=axis, keepdims=True)
    return (x - m) / jnp.sqrt(v + eps)

def _scatter_add(tgt, idx, src, axis=0):
    return tgt.at[idx].add(src)

def _segment_sum(src, seg, n):
    return jax.ops.segment_sum(src, seg, n)
kernel_name = 'mk_adj_preln_d1_adj_r2_539ac5'

def setup_inputs(seed: int=0):
    np.random.seed(seed)
    _w = jnp.asarray

    def _rec_inputs():
        import jax
        import jax.numpy as jnp
        _gk = jax.random.key(seed)
        x = -0.0002928 + 1 * jax.random.normal(jax.random.fold_in(_gk, 1), (4096, 256), jnp.float32)
        _a = jax.random.bernoulli(jax.random.fold_in(_gk, 2), 0.00390625, (4096, 4096))
        adj = _a.astype(jnp.int32)
        return (x, adj)
    x, adj = _rec_inputs()

    def _L0_gnn_setup():
        import jax, jax.numpy as jnp
        import numpy as np
        N = 4096
        IN_F = 256
        OUT_F = 256
        ALPHA = 0.2
        NEG_INF = -9000000000000000.0
        key = jax.random.key(seed)
        k1, k2, k3, k4, k5 = jax.random.split(key, 5)
        x = jax.random.normal(k1, (N, IN_F), dtype=jnp.float32)
        adj = jax.random.randint(k2, (N, N), 0, 2, dtype=jnp.int32)
        W = jax.random.normal(k3, (OUT_F, IN_F), dtype=jnp.float32) / np.sqrt(IN_F)
        a1 = jax.random.normal(k4, (OUT_F,), dtype=jnp.float32) / np.sqrt(2 * OUT_F)
        a2 = jax.random.normal(k5, (OUT_F,), dtype=jnp.float32) / np.sqrt(2 * OUT_F)
        return {'x': x, 'adj': adj, 'W': W, 'a1': a1, 'a2': a2}
    _L0_gnn_all = _L0_gnn_setup()
    _L0_gnn_in = {k: v for k, v in _L0_gnn_all.items() if k in ('W', 'a1', 'a2')}
    del _L0_gnn_all
    return {'x': x, 'adj': adj, 'L0_gnn_W': _L0_gnn_in['W'], 'L0_gnn_a1': _L0_gnn_in['a1'], 'L0_gnn_a2': _L0_gnn_in['a2']}

def reference(x, adj, L0_gnn_W, L0_gnn_a1, L0_gnn_a2):
    import jax
    import jax.numpy as jnp

    def _L0_gnn_ref(x, adj, W, a1, a2):
        import jax, jax.numpy as jnp
        import numpy as np
        N = 4096
        IN_F = 256
        OUT_F = 256
        ALPHA = 0.2
        NEG_INF = -9000000000000000.0
        h = x @ W.T
        src = h @ a1
        dst = h @ a2
        e = jax.nn.leaky_relu(src[:, None] + dst[None, :], negative_slope=ALPHA)
        e = jnp.where(adj == 0, jnp.float32(NEG_INF), e)
        attention = jax.nn.softmax(e, axis=1)
        h_prime = attention @ h
        return h_prime
    h = jnp.maximum(_layernorm(x, axis=-1), 0.0)
    x = x + _L0_gnn_ref(h, adj, L0_gnn_W, L0_gnn_a1, L0_gnn_a2)
    return x

_drawn_inputs = setup_inputs


def setup_inputs(seed=0):
    import zlib

    import numpy as np

    out = dict(_drawn_inputs(seed))
    spreads = {}
    factors = {'L0_gnn_a1': 4.192}
    for name, (base, spread) in spreads.items():
        noise = np.random.default_rng([zlib.crc32(name.encode()), seed]).standard_normal(out[name].shape)
        drawn = base * np.exp(spread * noise) if base else spread * noise
        out[name] = jnp.asarray(drawn.astype(out[name].dtype))
    for name, factor in factors.items():
        out[name] = (out[name] * factor).astype(out[name].dtype)
    return out
```

```python
import concourse.bass as bass
from concourse import mybir
from contextlib import ExitStack


def gat_layer(nc, x, adj_t, w, w_t, a1, a2, out):
    fp32, fp16, u32 = mybir.dt.float32, mybir.dt.float16, mybir.dt.uint32
    ALU, ACT, AX = mybir.AluOpType, mybir.ActivationFunctionType, mybir.AxisListType

    P = 128
    N, F = x.shape
    T = N // P
    KC = F // P
    FW = F + 2
    FD = F + 1
    EPS = 1e-5

    RB0 = 4
    RB = 7
    NG = (T - RB0) // RB
    assert RB0 + NG * RB == T
    W0, WG = RB0 * P, RB * P
    U = 8
    Q = T // U
    R = 4
    XB = 4
    CW = 512
    CB = CW // P

    HN_UP = 2.0 ** 11
    W_UP = 2.0 ** 15
    P_UP = 2.0 ** 15
    V_DOWN = 2.0 ** -15
    B_UP = 2.0 ** 14
    DEN_OVER_NUM = B_UP * V_DOWN / (HN_UP * W_UP * V_DOWN * V_DOWN)

    ctx = ExitStack()
    with ctx:
        def sb(name, shape, dt=fp32):
            return ctx.enter_context(nc.sbuf_tensor(name, shape, dt))

        def sem(name):
            return ctx.enter_context(nc.semaphore(name))

        x_sb = sb("x_sb", [P, T, F])
        h_sb = sb("h_sb", [P, T, FW])
        v_sb = sb("v_sb", [P, T, 2, F + 2], fp16)
        c_row = sb("c_row", [P, N])
        c_row0 = sb("c_row0", [P, W0])
        adj_sb = sb("adj_sb", [P, U, WG], u32)
        p_sb = sb("p_sb", [P, R, WG])
        p_hi = sb("p_hi", [P, R, WG], fp16)
        p_lo = sb("p_lo", [P, R, WG], fp16)
        out_sb = sb("out_sb", [P, RB, F])

        ident = sb("ident", [P, P])
        ones = sb("ones", [P, P])
        w_nat = sb("w_nat", [P, KC, F])
        w_f = sb("w_f", [P, KC, FW])
        w_hi = sb("w_hi", [P, KC, FW], fp16)
        w_lo = sb("w_lo", [P, KC, FW], fp16)
        a_sb = sb("a_sb", [P, KC, 2])
        squares = sb("squares", [P, KC, F])
        sumsq = sb("sumsq", [P, 2])
        norms = sb("norms", [P, 2])
        inv_norms = sb("inv_norms", [P, 2])
        w_scale = sb("w_scale", [P, 2])
        sd_scale = sb("sd_scale", [P, 1])
        den_scale = sb("den_scale", [P, 1])
        stats = sb("stats", [P, 2, nc.vector.BN_STATS_DIM])
        moments = sb("moments", [P, T, 2])
        eps_sb = sb("eps_sb", [P, 1])
        std = sb("std", [P, T])
        rstd = sb("rstd", [P, T])
        hn_sb = sb("hn_sb", [P, R, F])
        hnt_hi = sb("hnt_hi", [P, R, F], fp16)
        hnt_lo = sb("hnt_lo", [P, R, F], fp16)
        d_part = sb("d_part", [P, 1])
        d_one = sb("d_one", [1, 1])
        d_max = sb("d_max", [P, 1])
        t_col = sb("t_col", [P, T])
        dd_col = sb("dd_col", [P, T])
        c_col = sb("c_col", [P, T])
        g_col = sb("g_col", [P, T])
        b_col = sb("b_col", [P, T])
        bq_col = sb("bq_col", [P, T])
        diag = sb("diag", [P, CB, P])
        den = sb("den", [P, T])
        inv_den = sb("inv_den", [P, T])

        ps = ctx.enter_context(nc.psum_tensor("ps", [P, 8, 512], fp32))
        bank_w, bank_d, bank_c0 = 0, 1, 2
        bank_t, bank_h, bank_c = 4, 6, 4

        x_loaded = [sem(f"x_loaded{m}") for m in range(T // XB)]
        w_loaded = sem("w_loaded")
        adj_loaded = [sem(f"adj_loaded{u}") for u in range(U)]
        consts_ready = sem("consts_ready")
        dve_step = sem("dve_step")
        wa_done = sem("wa_done")
        sumsq_ready = sem("sumsq_ready")
        sumsq_summed = sem("sumsq_summed")
        norms_ready = sem("norms_ready")
        w_split = sem("w_split")
        moments_ready = sem("moments_ready")
        std_ready = sem("std_ready")
        hn_ready = sem("hn_ready")
        hn_turned = sem("hn_turned")
        hnt_hi_ready = sem("hnt_hi_ready")
        hnt_lo_ready = sem("hnt_lo_ready")
        h_done = sem("h_done")
        h_kept = sem("h_kept")
        d_part_ready = sem("d_part_ready")
        d_turned = sem("d_turned")
        d_one_ready = sem("d_one_ready")
        d_spread = sem("d_spread")
        t_ready = sem("t_ready")
        factors_ready = sem("factors_ready")
        b_ready = sem("b_ready")
        diag_ready = sem("diag_ready")
        c_spread = sem("c_spread")
        c_kept = sem("c_kept")
        v_hi_ready = sem("v_hi_ready")
        v_lo_ready = sem("v_lo_ready")
        weights_ready = sem("weights_ready")
        p_hi_ready = sem("p_hi_ready")
        p_lo_ready = sem("p_lo_ready")
        slot_free = sem("slot_free")
        rows_done = sem("rows_done")
        bank_free = sem("bank_free")
        out_ready = sem("out_ready")
        den_ready = sem("den_ready")
        inv_den_ready = sem("inv_den_ready")
        out_stored = [sem(f"out_stored{k}") for k in range(RB)]

        x_v = x.rearrange("(t p) f -> p t f", p=P)
        w_v = w.rearrange("(c p) k -> p c k", p=P)
        w_tv = w_t.rearrange("(c p) o -> p c o", p=P)
        out_v = out.rearrange("(t p) f -> p t f", p=P)
        edges = adj_t.bitcast(u32)

        block = ctx.enter_context(nc.Block())

        @block.sync
        def _(sp):
            sp.dma_start(x_sb[:, 0:XB, :], x_v[:, 0:XB, :]).then_inc(x_loaded[0], 16)
            sp.dma_start(w_nat[:], w_v).then_inc(w_loaded, 16)
            sp.dma_start(w_f[:, :, 0:F], w_tv).then_inc(w_loaded, 16)
            for n, a in enumerate((a1, a2)):
                sp.dma_start(a_sb[:, :, n], a.rearrange("(c p) -> p c", p=P),
                             allow_slow_non_contiguous=True).then_inc(w_loaded, 16)
            for m in range(1, T // XB):
                sp.dma_start(x_sb[:, m * XB:(m + 1) * XB, :], x_v[:, m * XB:(m + 1) * XB, :])\
                  .then_inc(x_loaded[m], 16)

            for u in range(U):
                sp.dma_start(adj_sb[:, u, 0:W0], edges[u * P:(u + 1) * P, 0:W0]).then_inc(adj_loaded[u], 16)
            with sp.Fori(1, Q) as q:
                for u in range(U):
                    sp.wait_ge(weights_ready, (q - 1) * U + (u + 1))
                    sp.dma_start(adj_sb[:, u, 0:W0], edges[bass.ds((q * U + u) * P, P), 0:W0])\
                      .then_inc(adj_loaded[u], 16)
            with sp.Fori(0, NG) as g:
                with sp.Fori(0, Q) as q:
                    for u in range(U):
                        sp.wait_ge(weights_ready, g * T + q * U + (T - U + u + 1))
                        sp.dma_start(adj_sb[:, u, :],
                                     edges[bass.ds((q * U + u) * P, P), bass.ds(g * WG + W0, WG)])\
                          .then_inc(adj_loaded[u], 16)

        @block.gpsimd
        def _(pool):
            nc.gpsimd.memset(ones[:], 1.0).then_inc(consts_ready, 1)
            nc.gpsimd.memset(eps_sb[:], EPS / HN_UP ** 2).then_inc(consts_ready, 1)
            pool.wait_ge(consts_ready, 2)
            nc.gpsimd.affine_select(out=ident[:], in_=ones[:], compare_op=ALU.is_equal, fill=0.0,
                                    base=0, pattern=[[-1, P]], channel_multiplier=1).then_inc(consts_ready, 1)

            for k in range(RB0):
                pool.wait_ge(out_ready, k + 1)
                pool.dma_start(out_v[:, k, :], out_sb[:, k, :]).then_inc(out_stored[k], 16)
            with pool.Fori(0, NG) as g:
                for k in range(RB):
                    pool.wait_ge(out_ready, g * RB + (RB0 + k + 1))
                    pool.dma_start(out_v[:, bass.ds(g * RB + (RB0 + k), 1), :], out_sb[:, k:k + 1, :])\
                        .then_inc(out_stored[k], 16)
            for k in range(RB):
                pool.wait_ge(out_stored[k], 16 * (NG + (k < RB0)))

        @block.scalar
        def _(act):
            act.wait_ge(sumsq_summed, 1)
            nc.scalar.activation(norms[:], ps[:, bank_w, 8:10], ACT.Sqrt).then_inc(norms_ready, 1)

            def std_of(m):
                act.wait_ge(moments_ready, (m + 1) * XB)
                nc.scalar.activation(std[:, m * XB:(m + 1) * XB], moments[:, m * XB:(m + 1) * XB, 1], ACT.Sqrt,
                                     bias=eps_sb[:, 0:1], scale=HN_UP ** -2).then_inc(std_ready, 1)

            def keep_h(t):
                act.wait_ge(h_done, t + 1)
                nc.scalar.activation(h_sb[:, t, :], ps[:, bank_h + t % 2, 0:FW], ACT.Copy).then_inc(h_kept, 1)

            act.wait_ge(consts_ready, 2)
            std_of(0)
            std_of(1)
            for t in range(T):
                act.wait_ge(hn_turned, t + 1)
                if t >= R:
                    act.wait_ge(h_done, t - R + 1)
                nc.scalar.activation(hnt_hi[:, t % R, :], ps[:, bank_t + t % 2, 0:F], ACT.Relu).then_inc(hnt_hi_ready, 1)
                if t >= 1:
                    keep_h(t - 1)
                if t % XB == XB - 1 and t // XB + 2 < T // XB:
                    std_of(t // XB + 2)
            keep_h(T - 1)

            act.wait_ge(t_ready, 1)
            nc.scalar.activation(c_col[:], t_col[:], ACT.Exp, scale=-0.8).then_inc(factors_ready, 1)
            act.wait_ge(t_ready, 2)
            nc.scalar.activation(g_col[:], dd_col[:], ACT.Exp, scale=0.8).then_inc(factors_ready, 1)
            nc.scalar.activation(b_col[:], dd_col[:], ACT.Exp, scale=0.2).then_inc(factors_ready, 1)
            act.wait_ge(c_spread, 1)
            nc.scalar.activation(c_row0[:], ps[:, bank_c0, :], ACT.Copy).then_inc(c_kept, 1)

            def split_hi(u, n, width):
                act.wait_ge(weights_ready, n + (u + 1))
                act.wait_ge(slot_free, n + (u + 1))
                nc.scalar.activation(p_hi[:, u % R, 0:width], p_sb[:, u % R, 0:width], ACT.Copy, scale=P_UP)\
                    .then_inc(p_hi_ready, 1)

            act.wait_ge(b_ready, 1)
            with act.Fori(0, Q) as q:
                for u in range(U):
                    t = q * U + u
                    nc.scalar.activation(v_sb[:, bass.ds(t, 1), 0, 0:F], h_sb[:, bass.ds(t, 1), 0:F], ACT.Copy,
                                         scale=bq_col[:, bass.ds(t, 1)]).then_inc(v_hi_ready, 1)
                    split_hi(u, q * U, W0)
                    if u % 4 == 2:
                        chunk = q * 2 + u // 4
                        act.wait_ge(c_spread, chunk + 2)
                        nc.scalar.activation(c_row[:, bass.ds(chunk * CW, CW)], ps[:, bank_c, :], ACT.Copy)\
                            .then_inc(c_kept, 1)
            with act.Fori(0, NG) as g:
                with act.Fori(0, Q) as q:
                    for u in range(U):
                        split_hi(u, g * T + q * U + T, WG)

        @block.vector
        def _(dve):
            steps = [0]

            def link(instruction):
                steps[0] += 1
                instruction.then_inc(dve_step, 1)
                dve.wait_ge(dve_step, steps[0])

            def moments_of(t):
                if t % XB == 0:
                    dve.wait_ge(x_loaded[t // XB], 16)
                link(nc.vector.bn_stats(stats[:, t % 2, :], x_sb[:, t, :]))
                nc.vector.bn_aggr(moments[:, t, :], stats[:, t % 2, :]).then_inc(moments_ready, 1)

            def rstd_of(m):
                dve.wait_ge(std_ready, m + 1)
                link(nc.vector.reciprocal(rstd[:, m * XB:(m + 1) * XB], std[:, m * XB:(m + 1) * XB]))

            def split_hn_lo(t):
                dve.wait_ge(hnt_hi_ready, t + 1)
                nc.vector.scalar_tensor_tensor(out=hnt_lo[:, t % R, :], in0=ps[:, bank_t + t % 2, 0:F], scalar=0.0,
                                               in1=hnt_hi[:, t % R, :], op0=ALU.max, op1=ALU.subtract)\
                    .then_inc(hnt_lo_ready, 1)

            for t in range(2 * XB):
                moments_of(t)

            dve.wait_ge(w_loaded, 64)
            dve.wait_ge(wa_done, 1)
            nc.vector.tensor_tensor_reduce(out=squares[:], in0=w_f[:, :, 0:F], in1=w_f[:, :, 0:F], scale=1.0, scalar=0.0,
                                           op0=ALU.mult, op1=ALU.add, accum_out=sumsq[:, 0:1])
            link(nc.vector.tensor_copy(w_f[:, :, F:FW], ps[:, bank_w, 0:2 * KC].rearrange("p (c n) -> p c n", c=KC)))
            nc.vector.tensor_tensor_reduce(out=squares[:, :, 0:2], in0=w_f[:, :, F:FW], in1=w_f[:, :, F:FW], scale=1.0,
                                           scalar=0.0, op0=ALU.mult, op1=ALU.add,
                                           accum_out=sumsq[:, 1:2]).then_inc(sumsq_ready, 1)
            dve.wait_ge(norms_ready, 1)
            link(nc.vector.tensor_scalar(norms[:], norms[:], 1e-15, None, ALU.max))
            link(nc.vector.reciprocal(inv_norms[:], norms[:]))
            link(nc.vector.tensor_scalar(w_scale[:], inv_norms[:], W_UP, None, ALU.mult))
            nc.vector.tensor_scalar(sd_scale[:], norms[:, 1:2], 1.0 / (HN_UP * W_UP), None, ALU.mult)
            link(nc.vector.tensor_scalar(den_scale[:], inv_norms[:, 0:1], 1.0 / 8.0, None, ALU.mult))
            for n, (a, b) in enumerate(((0, F), (F, FW))):
                link(nc.vector.tensor_scalar(w_hi[:, :, a:b], w_f[:, :, a:b], w_scale[:, n:n + 1], None, ALU.mult))
                last = nc.vector.scalar_tensor_tensor(out=w_lo[:, :, a:b], in0=w_f[:, :, a:b], scalar=w_scale[:, n:n + 1],
                                                      in1=w_hi[:, :, a:b], op0=ALU.mult, op1=ALU.subtract)
            last.then_inc(w_split, 1)

            rstd_of(0)
            for t in range(T):
                if t >= R:
                    dve.wait_ge(hn_turned, t - R + 1)
                nc.vector.tensor_scalar(hn_sb[:, t % R, :], x_sb[:, t, :], moments[:, t, 0:1], rstd[:, t:t + 1],
                                        ALU.subtract, ALU.mult).then_inc(hn_ready, 1)
                if t + 2 * XB < T:
                    moments_of(t + 2 * XB)
                if t >= 1:
                    split_hn_lo(t - 1)
                if t % XB == XB - 1 and t + 1 < T:
                    rstd_of(t // XB + 1)
            split_hn_lo(T - 1)

            dve.wait_ge(h_kept, T)
            link(nc.vector.tensor_reduce(d_part[:], h_sb[:, :, F + 1], AX.X, ALU.max))
            nc.vector.tensor_scalar(d_part[:], d_part[:], sd_scale[:, 0:1], None, ALU.mult).then_inc(d_part_ready, 1)
            dve.wait_ge(d_turned, 1)
            nc.vector.tensor_reduce(d_one[:], ps[0:1, bank_d, 0:P], AX.X, ALU.max).then_inc(d_one_ready, 1)
            nc.vector.tensor_scalar(t_col[:], h_sb[:, :, F], sd_scale[:, 0:1], None, ALU.mult)
            nc.vector.tensor_scalar(dd_col[:], h_sb[:, :, F + 1], sd_scale[:, 0:1], None, ALU.mult)
            dve.wait_ge(d_spread, 1)
            link(nc.vector.tensor_copy(d_max[:], ps[:, bank_d, P:P + 1]))
            nc.vector.tensor_scalar(t_col[:], t_col[:], d_max[:, 0:1], 0.0, ALU.add, ALU.max).then_inc(t_ready, 1)
            nc.vector.tensor_scalar(dd_col[:], dd_col[:], d_max[:, 0:1], None, ALU.subtract).then_inc(t_ready, 1)

            def diagonals(tiles):
                nc.vector.tensor_tensor(diag[:], ident[:, :].unsqueeze(1).to_broadcast([P, CB, P]),
                                        c_col[:, tiles].unsqueeze(2).to_broadcast([P, CB, P]), ALU.mult)\
                    .then_inc(diag_ready, 1)

            dve.wait_ge(factors_ready, 1)
            dve.wait_ge(consts_ready, 3)
            diagonals(slice(0, CB))
            dve.wait_ge(factors_ready, 3)
            nc.vector.tensor_scalar(bq_col[:], b_col[:], V_DOWN, None, ALU.mult).then_inc(b_ready, 1)
            link(nc.vector.tensor_scalar(v_sb[:, :, 0, F], b_col[:], B_UP, None, ALU.mult))
            link(nc.vector.scalar_tensor_tensor(out=v_sb[:, :, 1, F], in0=b_col[:], scalar=B_UP, in1=v_sb[:, :, 0, F],
                                                op0=ALU.mult, op1=ALU.subtract))

            def edge_weights(u, t, loads, c, width):
                dve.wait_ge(adj_loaded[u], loads)
                nc.vector.scalar_tensor_tensor(out=p_sb[:, u % R, 0:width], in0=c, scalar=g_col[:, bass.ds(t, 1)],
                                               in1=adj_sb[:, u, 0:width], op0=ALU.max, op1=ALU.min)\
                    .then_inc(weights_ready, 1)

            def split_lo(u, n, width):
                dve.wait_ge(p_hi_ready, n + (u + 1))
                nc.vector.scalar_tensor_tensor(out=p_lo[:, u % R, 0:width], in0=p_sb[:, u % R, 0:width], scalar=P_UP,
                                               in1=p_hi[:, u % R, 0:width], op0=ALU.mult, op1=ALU.subtract)\
                    .then_inc(p_lo_ready, 1)

            def values_lo(t):
                dve.wait_ge(v_hi_ready, t + 1)
                nc.vector.scalar_tensor_tensor(out=v_sb[:, bass.ds(t, 1), 1, 0:F], in0=h_sb[:, bass.ds(t, 1), 0:F],
                                               scalar=bq_col[:, bass.ds(t, 1)], in1=v_sb[:, bass.ds(t, 1), 0, 0:F],
                                               op0=ALU.mult, op1=ALU.subtract).then_inc(v_lo_ready, 1)

            def tiles_group0(q, first):
                for u in range(U):
                    edge_weights(u, q * U + u, (q + 1) * 16, c_row0[:], W0)
                    values_lo(q * U + u)
                    if u > 0 or not first:
                        split_lo(u - 1, q * U, W0)
                    if u % 4 == 0:
                        chunk = q * 2 + u // 4
                        dve.wait_ge(c_kept, chunk + 1)
                        diagonals(bass.ds(chunk * CB, CB))

            def tiles(g, q, first):
                for u in range(U):
                    edge_weights(u, q * U + u, g * (16 * Q) + (q + 1) * 16 + 16 * Q,
                                 c_row[:, bass.ds(g * WG + W0, WG)], WG)
                    if u > 0 or not first:
                        split_lo(u - 1, g * T + q * U + T, WG)

            def rows_out(k, b, done, stored, banks):
                if stored is not None:
                    dve.wait_ge(out_stored[k], stored)
                dve.wait_ge(rows_done, done)
                nc.vector.tensor_scalar(den[:, bass.ds(b, 1)], ps[:, k, F:FD], den_scale[:, 0:1], None, ALU.mult)\
                    .then_inc(den_ready, 1)
                dve.wait_ge(den_ready, done)
                nc.vector.reciprocal(inv_den[:, bass.ds(b, 1)], den[:, bass.ds(b, 1)]).then_inc(inv_den_ready, 1)
                dve.wait_ge(inv_den_ready, done)
                nc.vector.scalar_tensor_tensor(out=out_sb[:, k:k + 1, :], in0=ps[:, k:k + 1, 0:F],
                                               scalar=inv_den[:, bass.ds(b, 1)], in1=x_sb[:, bass.ds(b, 1), :],
                                               op0=ALU.mult, op1=ALU.add).then_inc(out_ready, 1)
                dve.wait_ge(out_ready, done)
                dve.sem_inc(bank_free, banks)

            dve.wait_ge(c_kept, 1)
            tiles_group0(0, True)
            with dve.Fori(1, Q) as q:
                tiles_group0(q, False)
            split_lo(U - 1, T - U, W0)
            for k in range(RB0):
                rows_out(k, k, k + 1, None, 1 if k < RB0 - 1 else RB - RB0 + 1)

            dve.wait_ge(c_kept, 2 * Q + 1)
            with dve.Fori(0, NG) as g:
                tiles(g, 0, True)
                with dve.Fori(1, Q) as q:
                    tiles(g, q, False)
                split_lo(U - 1, g * T + (2 * T - U), WG)
                for k in range(RB):
                    rows_out(k, g * RB + (RB0 + k), g * RB + (RB0 + k + 1), g * 16 + 16 * (k < RB0), 1)

        @block.tensor
        def _(pe):
            pe.sem_inc(slot_free, R)

            pe.wait_ge(w_loaded, 64)
            for c in range(KC):
                for o in range(KC):
                    last = nc.tensor.matmul(ps[:, bank_w, 2 * c:2 * c + 2], w_nat[:, o, c * P:(c + 1) * P], a_sb[:, o, :],
                                            start=(o == 0), stop=(o == KC - 1))
            last.then_inc(wa_done, 1)
            pe.wait_ge(consts_ready, 1)
            pe.wait_ge(sumsq_ready, 1)
            nc.tensor.matmul(ps[:, bank_w, 8:10], ones[:], sumsq[:], start=True, stop=True).then_inc(sumsq_summed, 1)

            def turn(t):
                pe.wait_ge(hn_ready, t + 1)
                if t >= 2:
                    pe.wait_ge(hnt_lo_ready, t - 1)
                for c in range(KC):
                    last = nc.tensor.transpose(ps[:, bank_t + t % 2, c * P:(c + 1) * P],
                                               hn_sb[:, t % R, c * P:(c + 1) * P], ident[:])
                last.then_inc(hn_turned, 1)

            def project(t):
                pe.wait_ge(hnt_hi_ready, t + 1)
                if t >= 2:
                    pe.wait_ge(h_kept, t - 1)
                o = ps[:, bank_h + t % 2, 0:FW]
                for c in range(KC):
                    a = hnt_hi[:, t % R, c * P:(c + 1) * P]
                    nc.tensor.matmul(o, a, w_hi[:, c, :], start=(c == 0), stop=False)
                    nc.tensor.matmul(o, a, w_lo[:, c, :], start=False, stop=False)
                pe.wait_ge(hnt_lo_ready, t + 1)
                for c in range(KC):
                    last = nc.tensor.matmul(o, hnt_lo[:, t % R, c * P:(c + 1) * P], w_hi[:, c, :],
                                            start=False, stop=(c == KC - 1))
                last.then_inc(h_done, 1)

            pe.wait_ge(consts_ready, 3)
            pe.wait_ge(w_split, 1)
            turn(0)
            for t in range(T):
                if t + 1 < T:
                    turn(t + 1)
                project(t)

            pe.wait_ge(d_part_ready, 1)
            nc.tensor.transpose(ps[0:1, bank_d, 0:P], d_part[:], ident[:]).then_inc(d_turned, 1)
            pe.wait_ge(d_one_ready, 1)
            nc.tensor.matmul(ps[:, bank_d, P:P + 1], ones[0:1, :], d_one[:], start=True, stop=True).then_inc(d_spread, 1)

            def spread_c(bank, chunks):
                pe.wait_ge(diag_ready, chunks)
                nc.tensor.matmul(ps[:, bank, :], ones[:], diag[:], start=True, stop=True).then_inc(c_spread, 1)

            spread_c(bank_c0, 1)

            def sums(u, t, n, blocks, first, last, freed, done):
                pe.wait_ge(p_hi_ready, n + (u + 1))
                for k in range(blocks):
                    a = p_hi[:, u % R, k * P:(k + 1) * P]
                    if first and freed is not None:
                        pe.wait_ge(bank_free, freed + (k + 1))
                    for part in range(2):
                        nc.tensor.matmul(ps[:, k, 0:FD], a, v_sb[:, bass.ds(t, 1), part, 0:FD],
                                         start=first and part == 0, stop=False, skip_group_check=True)
                pe.wait_ge(p_lo_ready, n + (u + 1))
                for k in range(blocks):
                    m = nc.tensor.matmul(ps[:, k, 0:FD], p_lo[:, u % R, k * P:(k + 1) * P],
                                         v_sb[:, bass.ds(t, 1), 0, 0:FD], start=False, stop=last, skip_group_check=True)
                    if last:
                        m.then_inc(rows_done, 1)
                    elif k == blocks - 1:
                        m.then_inc(slot_free, 1)
                if last:
                    pe.wait_ge(rows_done, done)
                    pe.sem_inc(slot_free, 1)

            def tiles_group0(q, first, last):
                for u in range(U):
                    if u % 4 == 1:
                        spread_c(bank_c, q * 2 + (u // 4 + 2))
                    pe.wait_ge(v_lo_ready, q * U + (u + 1))
                    sums(u, q * U + u, q * U, RB0, first and u == 0, last and u == U - 1, None, RB0)

            def tiles(g, q, first, last):
                for u in range(U):
                    sums(u, q * U + u, g * T + q * U + T, RB, first and u == 0, last and u == U - 1,
                         g * RB, g * RB + (RB0 + RB))

            tiles_group0(0, True, False)
            with pe.Fori(1, Q - 1) as q:
                tiles_group0(q, False, False)
            tiles_group0(Q - 1, False, True)
            pe.wait_ge(c_kept, 2 * Q + 1)
            with pe.Fori(0, NG) as g:
                tiles(g, 0, True, False)
                with pe.Fori(1, Q - 1) as q:
                    tiles(g, q, False, False)
                tiles(g, Q - 1, False, True)


def kernel(x, adj, L0_gnn_W, L0_gnn_a1, L0_gnn_a2):
    import numpy as np
    import concourse.bacc as bacc
    from concourse.bass_utils import run_bass_kernel_spmd as run

    w = np.asarray(L0_gnn_W)
    arrays = {
        "x": np.ascontiguousarray(x),
        "adj_t": np.ascontiguousarray(np.asarray(adj).T),
        "w": np.ascontiguousarray(w),
        "w_t": np.ascontiguousarray(w.T),
        "a1": np.ascontiguousarray(L0_gnn_a1),
        "a2": np.ascontiguousarray(L0_gnn_a2),
    }
    nc = bacc.Bacc("TRN2", target_bir_lowering=False, num_devices=1)
    args = [nc.dram_tensor(name, a.shape, mybir.dt.from_np(a.dtype), kind="ExternalInput").ap()
            for name, a in arrays.items()]
    out = nc.dram_tensor("out", arrays["x"].shape, mybir.dt.float32, kind="ExternalOutput").ap()
    gat_layer(nc, *args, out)
    return run(nc, [arrays], core_ids=[0]).results[0]["out"]
```

```python
import concourse.bass as bass
from concourse import mybir
from contextlib import ExitStack


def gat_layer(nc, x, adj_t, w, w_t, a1, a2, out):
    fp32, fp16, u32 = mybir.dt.float32, mybir.dt.float16, mybir.dt.uint32
    ALU, ACT, AX = mybir.AluOpType, mybir.ActivationFunctionType, mybir.AxisListType

    P = 128
    N, F = x.shape
    T = N // P
    KC = F // P
    FW = F + 2
    FD = F + 1
    EPS = 1e-5

    RB = 8
    NG = T // RB
    WG = RB * P
    HALF = RB // 2
    U = 8
    Q = T // U
    R = 4
    AHEAD = 2
    XB = 4
    CT = 512 // P
    CW = CT * P

    HN_UP = 2.0 ** 11
    W_UP = 2.0 ** 15
    P_UP = 2.0 ** 15
    V_DOWN = 2.0 ** -15
    B_UP = 2.0 ** 14
    DEN_OVER_NUM = B_UP * V_DOWN / (HN_UP * W_UP * V_DOWN * V_DOWN)

    ctx = ExitStack()
    with ctx:
        def sb(name, shape, dt=fp32):
            return ctx.enter_context(nc.sbuf_tensor(name, shape, dt))

        def sem(name):
            return ctx.enter_context(nc.semaphore(name))

        x_sb = sb("x_sb", [P, T, F])
        h_sb = sb("h_sb", [P, T, FW])
        v_sb = sb("v_sb", [P, T, 2, F + 2], fp16)
        c_row = sb("c_row", [P, N])
        adj_sb = sb("adj_sb", [P, R, WG], u32)
        p_sb = sb("p_sb", [P, R, WG])
        p_hi = sb("p_hi", [P, R, WG], fp16)
        p_lo = sb("p_lo", [P, R, WG], fp16)
        rows_sb = sb("rows_sb", [P, RB, FD])

        ident = sb("ident", [P, P])
        ones = sb("ones", [P, P])
        w_nat = sb("w_nat", [P, KC, F])
        w_f = sb("w_f", [P, KC, FW])
        w_hi = sb("w_hi", [P, KC, FW], fp16)
        w_lo = sb("w_lo", [P, KC, FW], fp16)
        a_sb = sb("a_sb", [P, KC, 2])
        squares = sb("squares", [P, KC, F])
        sumsq = sb("sumsq", [P, 2])
        norms = sb("norms", [P, 2])
        inv_norms = sb("inv_norms", [P, 2])
        w_scale = sb("w_scale", [P, 2])
        w1_hi = sb("w1_hi", [P, KC, P], fp16)
        w1_lo = sb("w1_lo", [P, KC, P], fp16)
        exp_scale = sb("exp_scale", [P, 3])
        exp_bias = sb("exp_bias", [P, 2])
        den_scale = sb("den_scale", [P, 1])
        stats = sb("stats", [P, T, nc.vector.BN_STATS_DIM])
        moments = sb("moments", [P, T, 2])
        eps_sb = sb("eps_sb", [P, 1])
        std = sb("std", [P, T])
        rstd = sb("rstd", [P, T])
        shift = sb("shift", [P, T])
        hn_sb = sb("hn_sb", [P, R, F])
        hnt_hi = sb("hnt_hi", [P, R, F], fp16)
        hnt_lo = sb("hnt_lo", [P, R, F], fp16)
        d_part = sb("d_part", [P, 1])
        d_one = sb("d_one", [1, 1])
        c_col = sb("c_col", [P, T])
        g_col = sb("g_col", [P, T])
        b_col = sb("b_col", [P, T])
        bq_col = sb("bq_col", [P, T])
        den = sb("den", [P, T])
        inv_den = sb("inv_den", [P, T])

        c_turned = sb("c_turned", [T, P])
        c_flat = nc.dram_tensor("c_flat", [T, P], fp32, kind="Internal").ap()
        ps = ctx.enter_context(nc.psum_tensor("ps", [P, 8, 512], fp32))
        bank_w, bank_d, bank_s = 0, 1, 2
        bank_t, bank_h = 4, 6

        x_loaded = [sem(f"x_loaded{m}") for m in range(T // XB)]
        w_loaded = sem("w_loaded")
        adj_loaded = [sem(f"adj_loaded{u}") for u in range(R)]
        consts_ready = sem("consts_ready")
        dve_step = sem("dve_step")
        wa_done = sem("wa_done")
        sumsq_ready = sem("sumsq_ready")
        sumsq_summed = sem("sumsq_summed")
        norms_ready = sem("norms_ready")
        w_split = sem("w_split")
        stats_ready = sem("stats_ready")
        moments_ready = sem("moments_ready")
        rstd_ready = sem("rstd_ready")
        std_ready = sem("std_ready")
        shift_ready = sem("shift_ready")
        hn_even_ready = sem("hn_even_ready")
        hn_odd_ready = sem("hn_odd_ready")
        hn_turned = sem("hn_turned")
        hnt_hi_ready = sem("hnt_hi_ready")
        hnt_lo_ready = sem("hnt_lo_ready")
        h_done = sem("h_done")
        h_kept = sem("h_kept")
        d_part_ready = sem("d_part_ready")
        d_turned = sem("d_turned")
        d_one_ready = sem("d_one_ready")
        d_spread = sem("d_spread")
        exp_bias_ready = sem("exp_bias_ready")
        g_ready = sem("g_ready")
        c_exp_ready = sem("c_exp_ready")
        c_col_exp_ready = sem("c_col_exp_ready")
        b_exp_ready = sem("b_exp_ready")
        c_col_ready = sem("c_col_ready")
        s_spread = sem("s_spread")
        b_ready = sem("b_ready")
        v_hi_ready = sem("v_hi_ready")
        v_lo_ready = sem("v_lo_ready")
        weights_ready = sem("weights_ready")
        p_hi_ready = sem("p_hi_ready")
        p_lo_ready = sem("p_lo_ready")
        slot_free = sem("slot_free")
        rows_done = sem("rows_done")
        rows_kept = sem("rows_kept")
        den_ready = sem("den_ready")
        inv_den_ready = sem("inv_den_ready")
        out_ready = sem("out_ready")
        last_stored = sem("last_stored")
        rows_free = sem("rows_free")
        c_all_turned = sem("c_all_turned")
        c_turned_kept = sem("c_turned_kept")
        c_flat_stored = sem("c_flat_stored")
        c_row_loaded = sem("c_row_loaded")
        out_stored = [sem(f"out_stored{k}") for k in range(RB)]

        x_v = x.rearrange("(t p) f -> p t f", p=P)
        w_v = w.rearrange("(c p) k -> p c k", p=P)
        w_tv = w_t.rearrange("(c p) o -> p c o", p=P)
        out_v = out.rearrange("(t p) f -> p t f", p=P)
        edges = adj_t.bitcast(u32)

        block = ctx.enter_context(nc.Block())

        @block.sync
        def _(sp):
            sp.dma_start(x_sb[:, 0:XB, :], x_v[:, 0:XB, :]).then_inc(x_loaded[0], 16)
            sp.dma_start(w_nat[:], w_v).then_inc(w_loaded, 16)
            sp.dma_start(w_f[:, :, 0:F], w_tv).then_inc(w_loaded, 16)
            for n, a in enumerate((a1, a2)):
                sp.dma_start(a_sb[:, :, n], a.rearrange("(c p) -> p c", p=P),
                             allow_slow_non_contiguous=True).then_inc(w_loaded, 16)
            for m in range(1, T // XB):
                sp.dma_start(x_sb[:, m * XB:(m + 1) * XB, :], x_v[:, m * XB:(m + 1) * XB, :])\
                  .then_inc(x_loaded[m], 16)

            def load_edges(u, t, g):
                sp.dma_start(adj_sb[:, u % R, :], edges[bass.ds(t * P, P), bass.ds(g * WG, WG)])\
                  .then_inc(adj_loaded[u % R], 16)

            def load_tiles(g, q, first):
                for u in range(U):
                    if u >= R or not first:
                        sp.wait_ge(weights_ready, g * T + q * U + (u - R + 1))
                    load_edges(u, q * U + u, g)

            load_tiles(0, 0, True)
            sp.wait_ge(c_turned_kept, 1)
            sp.dma_start(c_flat, c_turned[:]).then_inc(c_flat_stored, 16)
            sp.wait_ge(c_flat_stored, 16)
            sp.dma_start(c_row[:, WG:N], c_flat.rearrange("t p -> (t p)")[WG:N].partition_broadcast(P))\
              .then_inc(c_row_loaded, 16)
            with sp.Fori(1, Q) as q:
                load_tiles(0, q, False)
            with sp.Fori(1, NG) as g:
                with sp.Fori(0, Q) as q:
                    load_tiles(g, q, False)

            for k in range(RB):
                sp.wait_ge(out_ready, (NG - 1) * RB + k + 1)
                sp.dma_start(out_v[:, (NG - 1) * RB + k, :], rows_sb[:, k, 0:F]).then_inc(last_stored, 16)
            sp.wait_ge(last_stored, 16 * RB)

        @block.gpsimd
        def _(pool):
            nc.gpsimd.memset(ones[:], 1.0).then_inc(consts_ready, 1)
            nc.gpsimd.memset(eps_sb[:], EPS / HN_UP ** 2).then_inc(consts_ready, 1)
            pool.wait_ge(consts_ready, 2)
            nc.gpsimd.affine_select(out=ident[:], in_=ones[:], compare_op=ALU.is_equal, fill=0.0,
                                    base=0, pattern=[[-1, P]], channel_multiplier=1).then_inc(consts_ready, 1)

            pool.sem_inc(rows_free, RB)
            with pool.Fori(0, NG - 1) as g:
                for k in range(RB):
                    pool.wait_ge(out_ready, g * RB + (k + 1))
                    pool.dma_start(out_v[:, bass.ds(g * RB + k, 1), :], rows_sb[:, k:k + 1, 0:F])\
                        .then_inc(out_stored[k], 16)
                for k in range(RB):
                    pool.wait_ge(out_stored[k], g * 16 + 16)
                    pool.sem_inc(rows_free, 1)

        @block.scalar
        def _(act):
            def std_of(m):
                act.wait_ge(moments_ready, (m + 1) * XB)
                nc.scalar.activation(std[:, m * XB:(m + 1) * XB], moments[:, m * XB:(m + 1) * XB, 1], ACT.Sqrt,
                                     bias=eps_sb[:, 0:1], scale=HN_UP ** -2).then_inc(std_ready, 1)

            def keep_h(t):
                act.wait_ge(h_done, t + 1)
                nc.scalar.activation(h_sb[:, t, :], ps[:, bank_h + t % 2, 0:FW], ACT.Copy).then_inc(h_kept, 1)

            def normalise_odd(t):
                act.wait_ge(shift_ready, t // XB + 1)
                if t >= R:
                    act.wait_ge(hn_turned, t - R + 1)
                nc.scalar.activation(hn_sb[:, t % R, :], x_sb[:, t, :], ACT.Identity, bias=shift[:, t:t + 1],
                                     scale=rstd[:, t:t + 1]).then_inc(hn_odd_ready, 1)

            act.wait_ge(consts_ready, 2)
            std_of(0)
            act.wait_ge(sumsq_summed, 1)
            nc.scalar.activation(norms[:], ps[:, bank_w, 8:10], ACT.Sqrt).then_inc(norms_ready, 1)
            normalise_odd(1)
            std_of(1)
            for t in range(T):
                act.wait_ge(hn_turned, t + 1)
                if t >= R:
                    act.wait_ge(h_done, t - R + 1)
                nc.scalar.activation(hnt_hi[:, t % R, :], ps[:, bank_t + t % 2, 0:F], ACT.Relu).then_inc(hnt_hi_ready, 1)
                if t % 2 == 0 and t + 3 < T:
                    normalise_odd(t + 3)
                if t >= 1:
                    keep_h(t - 1)
                if t % XB == XB - 1 and t // XB + 2 < T // XB:
                    std_of(t // XB + 2)
            keep_h(T - 1)

            act.wait_ge(exp_bias_ready, 1)
            for m in range(WG // CW):
                act.wait_ge(s_spread, (m + 1) * CT)
                nc.scalar.activation(c_row[:, m * CW:(m + 1) * CW], ps[:, bank_s + m, :], ACT.Exp,
                                     bias=exp_bias[:, 0:1], scale=exp_scale[:, 0:1]).then_inc(c_exp_ready, 1)
                if m == 0:
                    nc.scalar.activation(g_col[:], h_sb[:, :, F + 1], ACT.Exp, bias=exp_bias[:, 0:1],
                                         scale=exp_scale[:, 1:2]).then_inc(g_ready, 1)
            nc.scalar.activation(b_col[:], h_sb[:, :, F + 1], ACT.Exp, bias=exp_bias[:, 1:2],
                                 scale=exp_scale[:, 2:3]).then_inc(b_exp_ready, 1)
            nc.scalar.activation(c_col[:], h_sb[:, :, F], ACT.Exp, bias=exp_bias[:, 0:1],
                                 scale=exp_scale[:, 0:1]).then_inc(c_col_exp_ready, 1)
            act.wait_ge(c_all_turned, 1)
            nc.scalar.activation(c_turned[:], ps[0:T, bank_w, 0:P], ACT.Copy).then_inc(c_turned_kept, 1)

            def split_hi(u, n):
                act.wait_ge(weights_ready, n + (u + 1))
                act.wait_ge(slot_free, n + (u + 1))
                nc.scalar.activation(p_hi[:, u % R, :], p_sb[:, u % R, :], ACT.Copy, scale=P_UP)\
                    .then_inc(p_hi_ready, 1)

            def keep_rows(g):
                for k in range(RB):
                    act.wait_ge(rows_free, g * RB + (k + 1))
                    act.wait_ge(rows_done, g * RB + (k + 1))
                    nc.scalar.activation(rows_sb[:, k, :], ps[:, k, 0:FD], ACT.Copy).then_inc(rows_kept, 1)

            act.wait_ge(b_ready, 1)
            with act.Fori(0, Q) as q:
                for u in range(U):
                    t = q * U + u
                    nc.scalar.activation(v_sb[:, bass.ds(t, 1), 0, 0:F], h_sb[:, bass.ds(t, 1), 0:F], ACT.Copy,
                                         scale=bq_col[:, bass.ds(t, 1)]).then_inc(v_hi_ready, 1)
                    split_hi(u, q * U)
            with act.Fori(1, NG) as g:
                for u in range(U):
                    if u == AHEAD:
                        keep_rows(g - 1)
                    split_hi(u, g * T)
                with act.Fori(1, Q) as q:
                    for u in range(U):
                        split_hi(u, g * T + q * U)

        @block.vector
        def _(dve):
            steps = [0]

            def link(instruction):
                steps[0] += 1
                instruction.then_inc(dve_step, 1)
                dve.wait_ge(dve_step, steps[0])

            def stats_of(t):
                if t % XB == 0:
                    dve.wait_ge(x_loaded[t // XB], 16)
                nc.vector.bn_stats(stats[:, t, :], x_sb[:, t, :]).then_inc(stats_ready, 1)

            def gather(t):
                dve.wait_ge(stats_ready, t + 1)
                nc.vector.bn_aggr(moments[:, t, :], stats[:, t, :]).then_inc(moments_ready, 1)

            def rstd_of(m):
                dve.wait_ge(std_ready, m + 1)
                batch = slice(m * XB, (m + 1) * XB)
                nc.vector.reciprocal(rstd[:, batch], std[:, batch]).then_inc(rstd_ready, 1)
                dve.wait_ge(rstd_ready, m + 1)
                nc.vector.scalar_tensor_tensor(out=shift[:, batch], in0=moments[:, batch, 0], scalar=-1.0,
                                               in1=rstd[:, batch], op0=ALU.mult, op1=ALU.mult).then_inc(shift_ready, 1)

            def split_hn_lo(t):
                dve.wait_ge(hnt_hi_ready, t + 1)
                nc.vector.scalar_tensor_tensor(out=hnt_lo[:, t % R, :], in0=ps[:, bank_t + t % 2, 0:F], scalar=0.0,
                                               in1=hnt_hi[:, t % R, :], op0=ALU.max, op1=ALU.subtract)\
                    .then_inc(hnt_lo_ready, 1)

            def normalise_even(t):
                if t >= R:
                    dve.wait_ge(hn_turned, t - R + 1)
                nc.vector.tensor_scalar(hn_sb[:, t % R, :], x_sb[:, t, :], moments[:, t, 0:1], rstd[:, t:t + 1],
                                        ALU.subtract, ALU.mult).then_inc(hn_even_ready, 1)

            def moments_of_batch(m):
                for t in range(m * XB, (m + 1) * XB):
                    stats_of(t)
                    if t > m * XB:
                        gather(t - 1)
                gather(t)

            moments_of_batch(0)

            dve.wait_ge(w_loaded, 64)
            dve.wait_ge(wa_done, 1)
            nc.vector.tensor_tensor_reduce(out=squares[:], in0=w_f[:, :, 0:F], in1=w_f[:, :, 0:F], scale=1.0, scalar=0.0,
                                           op0=ALU.mult, op1=ALU.add, accum_out=sumsq[:, 0:1])
            link(nc.vector.tensor_copy(w_f[:, :, F:FW], ps[:, bank_w, 0:2 * KC].rearrange("p (c n) -> p c n", c=KC)))
            nc.vector.tensor_tensor_reduce(out=squares[:, :, 0:2], in0=w_f[:, :, F:FW], in1=w_f[:, :, F:FW], scale=1.0,
                                           scalar=0.0, op0=ALU.mult, op1=ALU.add,
                                           accum_out=sumsq[:, 1:2]).then_inc(sumsq_ready, 1)
            dve.wait_ge(norms_ready, 1)
            link(nc.vector.tensor_scalar(norms[:], norms[:], 1e-15, None, ALU.max))
            link(nc.vector.reciprocal(inv_norms[:], norms[:]))
            link(nc.vector.tensor_scalar(w_scale[:], inv_norms[:], W_UP, None, ALU.mult))
            for n, factor in enumerate((-0.8, 0.8, 0.2)):
                nc.vector.tensor_scalar(exp_scale[:, n:n + 1], norms[:, 1:2], factor / (HN_UP * W_UP), None, ALU.mult)
            link(nc.vector.tensor_scalar(den_scale[:], inv_norms[:, 0:1], 1.0 / 8.0, None, ALU.mult))
            for n, (a, b) in enumerate(((0, F), (F, FW))):
                link(nc.vector.tensor_scalar(w_hi[:, :, a:b], w_f[:, :, a:b], w_scale[:, n:n + 1], None, ALU.mult))
                last = nc.vector.scalar_tensor_tensor(out=w_lo[:, :, a:b], in0=w_f[:, :, a:b], scalar=w_scale[:, n:n + 1],
                                                      in1=w_hi[:, :, a:b], op0=ALU.mult, op1=ALU.subtract)
            link(last)
            nc.vector.tensor_copy(w1_hi[:], w_hi[:, :, F:F + 1].to_broadcast([P, KC, P]))
            nc.vector.tensor_copy(w1_lo[:], w_lo[:, :, F:F + 1].to_broadcast([P, KC, P])).then_inc(w_split, 1)

            moments_of_batch(1)
            rstd_of(0)
            normalise_even(0)
            normalise_even(2)
            for t in range(T):
                if t % XB == 0 and t + XB < T:
                    rstd_of(t // XB + 1)
                if t % 2 == 1 and t + 3 < T:
                    normalise_even(t + 3)
                if t + 2 * XB < T:
                    stats_of(t + 2 * XB)
                if t >= 1:
                    split_hn_lo(t - 1)
                if t + 2 * XB < T:
                    gather(t + 2 * XB)
            split_hn_lo(T - 1)

            dve.wait_ge(h_kept, T)
            nc.vector.tensor_reduce(d_part[:], h_sb[:, :, F + 1], AX.X, ALU.max).then_inc(d_part_ready, 1)
            dve.wait_ge(d_turned, 1)
            nc.vector.tensor_reduce(d_one[:], ps[0:1, bank_d, 0:P], AX.X, ALU.max).then_inc(d_one_ready, 1)
            dve.wait_ge(d_spread, 1)
            nc.vector.tensor_scalar(exp_bias[:, 1:2], exp_scale[:, 2:3], ps[:, bank_d, P:P + 1], -1.0, ALU.mult, ALU.mult)
            nc.vector.tensor_scalar(exp_bias[:, 0:1], exp_scale[:, 0:1], ps[:, bank_d, P:P + 1], None, ALU.mult)\
                .then_inc(exp_bias_ready, 1)

            for m in range(WG // CW):
                dve.wait_ge(c_exp_ready, m + 1)
                first = c_row[:, m * CW:(m + 1) * CW]
                link(nc.vector.tensor_scalar(first, first, 1.0, None, ALU.min))
            dve.wait_ge(b_exp_ready, 1)
            nc.vector.tensor_scalar(bq_col[:], b_col[:], V_DOWN, None, ALU.mult).then_inc(b_ready, 1)
            link(nc.vector.tensor_scalar(v_sb[:, :, 0, F], b_col[:], B_UP, None, ALU.mult))
            link(nc.vector.scalar_tensor_tensor(out=v_sb[:, :, 1, F], in0=b_col[:], scalar=B_UP, in1=v_sb[:, :, 0, F],
                                                op0=ALU.mult, op1=ALU.subtract))
            dve.wait_ge(c_col_exp_ready, 1)
            nc.vector.tensor_scalar(c_col[:], c_col[:], 1.0, None, ALU.min).then_inc(c_col_ready, 1)
            dve.wait_ge(g_ready, 1)

            def edge_weights(u, t, loads, g):
                dve.wait_ge(adj_loaded[u % R], loads)
                nc.vector.scalar_tensor_tensor(out=p_sb[:, u % R, :], in0=c_row[:, bass.ds(g * WG, WG)],
                                               scalar=g_col[:, bass.ds(t, 1)], in1=adj_sb[:, u % R, :],
                                               op0=ALU.max, op1=ALU.min).then_inc(weights_ready, 1)

            def split_lo(u, n):
                dve.wait_ge(p_hi_ready, n + (u + 1))
                nc.vector.scalar_tensor_tensor(out=p_lo[:, u % R, :], in0=p_sb[:, u % R, :], scalar=P_UP,
                                               in1=p_hi[:, u % R, :], op0=ALU.mult, op1=ALU.subtract)\
                    .then_inc(p_lo_ready, 1)

            def values_lo(t):
                dve.wait_ge(v_hi_ready, t + 1)
                nc.vector.scalar_tensor_tensor(out=v_sb[:, bass.ds(t, 1), 1, 0:F], in0=h_sb[:, bass.ds(t, 1), 0:F],
                                               scalar=bq_col[:, bass.ds(t, 1)], in1=v_sb[:, bass.ds(t, 1), 0, 0:F],
                                               op0=ALU.mult, op1=ALU.subtract).then_inc(v_lo_ready, 1)

            def inverses(g, half):
                a = half * HALF
                dve.wait_ge(rows_kept, g * RB + (a + HALF))
                nc.vector.tensor_scalar(den[:, bass.ds(g * RB + a, HALF)], rows_sb[:, a:a + HALF, F], den_scale[:, 0:1],
                                        None, ALU.mult).then_inc(den_ready, 1)
                dve.wait_ge(den_ready, g * 2 + (half + 1))
                nc.vector.reciprocal(inv_den[:, bass.ds(g * RB + a, HALF)], den[:, bass.ds(g * RB + a, HALF)])\
                    .then_inc(inv_den_ready, 1)
                dve.wait_ge(inv_den_ready, g * 2 + (half + 1))

            def rows_out(g, k):
                b = g * RB + k
                nc.vector.scalar_tensor_tensor(out=rows_sb[:, k:k + 1, 0:F], in0=rows_sb[:, k:k + 1, 0:F],
                                               scalar=inv_den[:, bass.ds(b, 1)], in1=x_sb[:, bass.ds(b, 1), :],
                                               op0=ALU.mult, op1=ALU.add).then_inc(out_ready, 1)

            def tiles_group0(q, first):
                for u in range(U):
                    edge_weights(u, q * U + u, q * 32 + 16 * (u // R + 1), 0)
                    values_lo(q * U + u)
                    if u > 0 or not first:
                        split_lo(u - 1, q * U)

            def tiles(g, q, first):
                for u in range(U):
                    edge_weights(u, q * U + u, g * (32 * Q) + q * 32 + 16 * (u // R + 1), g)
                    if u > 0 or not first:
                        split_lo(u - 1, g * T + q * U)
                    if first and AHEAD < u <= AHEAD + RB // 2:
                        if (u - AHEAD - 1) % 2 == 0:
                            inverses(g - 1, (u - AHEAD - 1) // 2)
                        for k in range(2 * (u - AHEAD - 1), 2 * (u - AHEAD)):
                            rows_out(g - 1, k)

            tiles_group0(0, True)
            with dve.Fori(1, Q) as q:
                tiles_group0(q, False)
            split_lo(U - 1, T - U)
            dve.wait_ge(c_row_loaded, 16)
            with dve.Fori(1, NG) as g:
                tiles(g, 0, True)
                with dve.Fori(1, Q) as q:
                    tiles(g, q, False)
                split_lo(U - 1, g * T + (T - U))
            for k in range(RB):
                b = (NG - 1) * RB + k
                dve.wait_ge(rows_done, b + 1)
                link(nc.vector.tensor_scalar(den[:, b:b + 1], ps[:, k, F:FD], den_scale[:, 0:1], None, ALU.mult))
                link(nc.vector.reciprocal(inv_den[:, b:b + 1], den[:, b:b + 1]))
                if k == 0:
                    dve.wait_ge(rows_free, (NG - 1) * RB + RB)
                nc.vector.scalar_tensor_tensor(out=rows_sb[:, k, 0:F], in0=ps[:, k, 0:F], scalar=inv_den[:, b:b + 1],
                                               in1=x_sb[:, b, :], op0=ALU.mult, op1=ALU.add).then_inc(out_ready, 1)

        @block.tensor
        def _(pe):
            pe.sem_inc(slot_free, R)

            pe.wait_ge(w_loaded, 64)
            for c in range(KC):
                for o in range(KC):
                    last = nc.tensor.matmul(ps[:, bank_w, 2 * c:2 * c + 2], w_nat[:, o, c * P:(c + 1) * P], a_sb[:, o, :],
                                            start=(o == 0), stop=(o == KC - 1))
            last.then_inc(wa_done, 1)
            pe.wait_ge(consts_ready, 1)
            pe.wait_ge(sumsq_ready, 1)
            nc.tensor.matmul(ps[:, bank_w, 8:10], ones[:], sumsq[:], start=True, stop=True).then_inc(sumsq_summed, 1)

            def turn(t):
                pe.wait_ge(hn_odd_ready if t % 2 else hn_even_ready, t // 2 + 1)
                if t >= 2:
                    pe.wait_ge(hnt_lo_ready, t - 1)
                for c in range(KC):
                    last = nc.tensor.transpose(ps[:, bank_t + t % 2, c * P:(c + 1) * P],
                                               hn_sb[:, t % R, c * P:(c + 1) * P], ident[:])
                last.then_inc(hn_turned, 1)

            def project(t):
                pe.wait_ge(hnt_hi_ready, t + 1)
                if t >= 2:
                    pe.wait_ge(h_kept, t - 1)
                o = ps[:, bank_h + t % 2, 0:FW]
                for c in range(KC):
                    a = hnt_hi[:, t % R, c * P:(c + 1) * P]
                    nc.tensor.matmul(o, a, w_hi[:, c, :], start=(c == 0), stop=False)
                    nc.tensor.matmul(o, a, w_lo[:, c, :], start=False, stop=False)
                pe.wait_ge(hnt_lo_ready, t + 1)
                for c in range(KC):
                    last = nc.tensor.matmul(o, hnt_lo[:, t % R, c * P:(c + 1) * P], w_hi[:, c, :],
                                            start=False, stop=(c == KC - 1))
                last.then_inc(h_done, 1)

            def spread_s(t):
                o = ps[:, bank_s + t // CT, (t % CT) * P:(t % CT + 1) * P]
                for c in range(KC):
                    hi, lo = (part[:, t % R, c * P:(c + 1) * P] for part in (hnt_hi, hnt_lo))
                    nc.tensor.matmul(o, w1_hi[:, c, :], hi, start=(c == 0), stop=False)
                    nc.tensor.matmul(o, w1_lo[:, c, :], hi, start=False, stop=False)
                    last = nc.tensor.matmul(o, w1_hi[:, c, :], lo, start=False, stop=(c == KC - 1))
                last.then_inc(s_spread, 1)

            pe.wait_ge(consts_ready, 3)
            turn(0)
            pe.wait_ge(w_split, 1)
            for t in range(T):
                if t + 1 < T:
                    turn(t + 1)
                project(t)
                if t < RB:
                    spread_s(t)

            pe.wait_ge(d_part_ready, 1)
            nc.tensor.transpose(ps[0:1, bank_d, 0:P], d_part[:], ident[:]).then_inc(d_turned, 1)
            pe.wait_ge(d_one_ready, 1)
            nc.tensor.matmul(ps[:, bank_d, P:P + 1], ones[0:1, :], d_one[:], start=True, stop=True).then_inc(d_spread, 1)

            pe.wait_ge(c_col_ready, 1)
            nc.tensor.transpose(ps[0:T, bank_w, 0:P], c_col[:], ident[:]).then_inc(c_all_turned, 1)

            def product(u, t, k, part, v, start, stop):
                return nc.tensor.matmul(ps[:, k, 0:FD], part[:, u % R, k * P:(k + 1) * P], v_sb[:, bass.ds(t, 1), v, 0:FD],
                                        start=start, stop=stop, skip_group_check=True)

            def sums(u, t, n, g, first):
                pe.wait_ge(p_hi_ready, n + (u + 1))
                for k in range(RB):
                    if first and g is not None:
                        pe.wait_ge(rows_kept, (g - 1) * RB + (k + 1))
                    product(u, t, k, p_hi, 0, first, False)
                    product(u, t, k, p_hi, 1, False, False)
                pe.wait_ge(p_lo_ready, n + (u + 1))
                for k in range(RB):
                    done = product(u, t, k, p_lo, 0, False, False)
                done.then_inc(slot_free, 1)

            def last_sums(t, n, g):
                pe.wait_ge(p_lo_ready, n + U)
                for k in range(RB):
                    for u in (U - 2, U - 1):
                        product(u, t + u, k, p_hi, 0, False, False)
                        product(u, t + u, k, p_hi, 1, False, False)
                        done = product(u, t + u, k, p_lo, 0, False, u == U - 1)
                    done.then_inc(rows_done, 1)
                pe.wait_ge(rows_done, (g + 1) * RB)
                pe.sem_inc(slot_free, 2)

            def tiles(g, q, first, last):
                n = q * U if g is None else g * T + q * U
                for u in range(U - 2 if last else U):
                    if g is None:
                        pe.wait_ge(v_lo_ready, q * U + (u + 1))
                    sums(u, q * U + u, n, g, first and u == 0)
                if last:
                    if g is None:
                        pe.wait_ge(v_lo_ready, T)
                    last_sums(q * U, n, 0 if g is None else g)

            def group(g):
                tiles(g, 0, True, False)
                with pe.Fori(1, Q - 1) as q:
                    tiles(g, q, False, False)
                tiles(g, Q - 1, False, True)

            pe.wait_ge(c_turned_kept, 1)
            group(None)
            with pe.Fori(1, NG) as g:
                group(g)


def kernel(x, adj, L0_gnn_W, L0_gnn_a1, L0_gnn_a2):
    import numpy as np
    import concourse.bacc as bacc
    from concourse.bass_utils import run_bass_kernel_spmd as run

    w = np.asarray(L0_gnn_W)
    arrays = {
        "x": np.ascontiguousarray(x),
        "adj_t": np.ascontiguousarray(np.asarray(adj).T),
        "w": np.ascontiguousarray(w),
        "w_t": np.ascontiguousarray(w.T),
        "a1": np.ascontiguousarray(L0_gnn_a1),
        "a2": np.ascontiguousarray(L0_gnn_a2),
    }
    nc = bacc.Bacc("TRN2", target_bir_lowering=False, num_devices=1)
    args = [nc.dram_tensor(name, a.shape, mybir.dt.from_np(a.dtype), kind="ExternalInput").ap()
            for name, a in arrays.items()]
    out = nc.dram_tensor("out", arrays["x"].shape, mybir.dt.float32, kind="ExternalOutput").ap()
    gat_layer(nc, *args, out)
    return run(nc, [arrays], core_ids=[0]).results[0]["out"]
```

```python
import concourse.bass as bass
from concourse import mybir
from contextlib import ExitStack
import math


def gat_layer(nc, x, adj, adj_t, w, w_t, a1, a2, out):
    fp32, fp16, u32 = mybir.dt.float32, mybir.dt.float16, mybir.dt.uint32
    ALU, ACT, AX = mybir.AluOpType, mybir.ActivationFunctionType, mybir.AxisListType

    P = 128
    N, F = x.shape
    T = N // P
    KC = F // P
    FW = F + 2
    FD = F + 1
    EPS = 1e-5

    W_PARTS = (slice(0, F), slice(F, FW))
    RB = 8
    NG = T // RB
    WG = RB * P
    HALF = RB // 2
    U = 8
    Q = T // U
    R = 4
    AHEAD = 2
    BUSY_START, BUSY_SPLIT, BUSY_C = 6, 8, 5
    XB = 4
    CT = 512 // P
    CW = CT * P
    FIRST_PARTS = ((0, 2), (2, 4), (4, 8))
    BY_VECTOR = [0, 2] + list(range(4, T, 4))
    BY_SCALAR = [1] + sorted([*range(5, T, 4), *range(6, T, 4)])
    BY_GPSIMD = list(range(3, T, 4))
    RN = 8

    HN_UP = 2.0 ** 11
    W_UP = 2.0 ** 15
    P_UP = 2.0 ** 15
    H_DOWN = 2.0 ** -15
    ONE_UP = 2.0 ** 14
    DEN_LOW = 2.0 ** -6 * P_UP * ONE_UP
    DEN_TINY = 1e-30
    NEG_INF = -9e15
    SLOPE = 0.2
    GC = 4
    H_UP = HN_UP * W_UP * H_DOWN

    ctx = ExitStack()
    with ctx:
        def sb(name, shape, dt=fp32):
            return ctx.enter_context(nc.sbuf_tensor(name, shape, dt))

        def sem(name):
            return ctx.enter_context(nc.semaphore(name))

        x_sb = sb("x_sb", [P, T, F])
        h_sb = sb("h_sb", [P, T, FW])
        v_sb = sb("v_sb", [P, T, 2, F + 2], fp16)
        c_row = sb("c_row", [P, N])
        adj_sb = sb("adj_sb", [P, R, WG], u32)
        p_sb = sb("p_sb", [P, R, WG])
        p_hi = sb("p_hi", [P, R, WG], fp16)
        p_lo = sb("p_lo", [P, R, WG], fp16)
        rows_sb = sb("rows_sb", [P, RB, FD])

        ident = sb("ident", [P, P])
        ones = sb("ones", [P, P])
        w_nat = sb("w_nat", [P, KC, F])
        w_f = sb("w_f", [P, KC, FW])
        w_hi = sb("w_hi", [P, KC, FW], fp16)
        w_lo = sb("w_lo", [P, KC, FW], fp16)
        a_sb = sb("a_sb", [P, KC, 2])
        squares = sb("squares", [P, KC, F])
        squares_a = sb("squares_a", [P, KC, 2])
        sumsq = sb("sumsq", [P, 2])
        norms = sb("norms", [P, 2])
        inv_norms = sb("inv_norms", [P, 2])
        w_scale = sb("w_scale", [P, 2])
        w1_hi = sb("w1_hi", [P, KC, P], fp16)
        w1_lo = sb("w1_lo", [P, KC, P], fp16)
        exp_scale = sb("exp_scale", [P, 5])
        exp_bias = sb("exp_bias", [P, 2])
        den_scale = sb("den_scale", [P, 1])
        stats = sb("stats", [P, T, nc.vector.BN_STATS_DIM])
        moments = sb("moments", [P, T, 2])
        eps_sb = sb("eps_sb", [P, 1])
        std = sb("std", [P, T])
        rstd = sb("rstd", [P, T])
        shift = sb("shift", [P, T])
        hn_sb = sb("hn_sb", [P, RN, F])
        hnt_hi = sb("hnt_hi", [P, KC, R * P], fp16)
        hnt_lo = sb("hnt_lo", [P, KC, R * P], fp16)
        first_hi = sb("first_hi", [P, KC, WG], fp16)
        first_lo = sb("first_lo", [P, KC, WG], fp16)
        d_most = sb("d_most", [P, 1])
        d_part = sb("d_part", [P, 1])
        d_one = sb("d_one", [1, 1])
        c_col = sb("c_col", [P, T])
        g_col = sb("g_col", [P, T])
        p_scale = sb("p_scale", [P, T])
        t_row = rows_sb[:].rearrange("p k f -> p (k f)")
        t_col = sb("t_col", [P, T])
        up_row = sb("up_row", [1, P])
        warm = sb("warm", [P, 1])
        den = sb("den", [P, T])
        inv_den = sb("inv_den", [P, T])

        c_turned = sb("c_turned", [T, P])
        den_least = sb("den_least", [P, 1])
        den_low = sb("den_low", [P, 1])
        den_is_low = sb("den_is_low", [P, 1])
        plain_needed = sb("plain_needed", [1, 1], mybir.dt.int32)
        unit = sb("unit", [P, 1])
        s_col = sb("s_col", [P, T])
        d_col = sb("d_col", [P, T])
        row_max = sb("row_max", [P, 2])
        row_sum = sb("row_sum", [P, 1])
        row_inv = sb("row_inv", [P, 2])
        c_flat = nc.dram_tensor("c_flat", [T, P], fp32, kind="Internal").ap()
        ps = ctx.enter_context(nc.psum_tensor("ps", [P, 8, 512], fp32))
        bank_w, bank_d, bank_s = 0, 1, 2
        bank_h = 6
        banks_t = (4, 5, 1, 0)
        turned_c = slice(512 - P, 512)

        x_loaded = [sem(f"x_loaded{m}") for m in range(T // XB)]
        w_nat_loaded = sem("w_nat_loaded")
        w_t_loaded = sem("w_t_loaded")
        adj_loaded = [sem(f"adj_loaded{u}") for u in range(R)]
        consts_ready = sem("consts_ready")
        dve_step = sem("dve_step")
        wa_done = sem("wa_done")
        sumsq_ready = sem("sumsq_ready")
        sumsq_summed = sem("sumsq_summed")
        wa_kept = sem("wa_kept")
        norms_ready = sem("norms_ready")
        w_scale_ready = sem("w_scale_ready")
        w_hi_ready = sem("w_hi_ready")
        part_weights_ready = sem("part_weights_ready")
        part_hi_ready = sem("part_hi_ready")
        w_lo_ready = sem("w_lo_ready")
        w1_ready = sem("w1_ready")
        stats_ready = sem("stats_ready")
        moments_ready = sem("moments_ready")
        rstd_ready = sem("rstd_ready")
        std_ready = sem("std_ready")
        shift_ready = sem("shift_ready")
        hn_vector_ready = sem("hn_vector_ready")
        hn_scalar_ready = sem("hn_scalar_ready")
        hn_gpsimd_ready = sem("hn_gpsimd_ready")
        hn_turned = sem("hn_turned")
        hnt_hi_ready = sem("hnt_hi_ready")
        hnt_lo_ready = sem("hnt_lo_ready")
        h_done = sem("h_done")
        h_kept = sem("h_kept")
        d_part_ready = sem("d_part_ready")
        d_turned = sem("d_turned")
        d_one_ready = sem("d_one_ready")
        d_spread = sem("d_spread")
        exp_bias_ready = sem("exp_bias_ready")
        g_ready = sem("g_ready")
        t_row_ready = sem("t_row_ready")
        t_col_ready = sem("t_col_ready")
        c_exp_ready = sem("c_exp_ready")
        c_col_ready = sem("c_col_ready")
        s_spread = sem("s_spread")
        p_scale_ready = sem("p_scale_ready")
        v_hi_ready = sem("v_hi_ready")
        v_lo_ready = sem("v_lo_ready")
        v_ones_ready = sem("v_ones_ready")
        weights_ready = sem("weights_ready")
        p_hi_ready = sem("p_hi_ready")
        p_lo_ready = sem("p_lo_ready")
        slot_free = sem("slot_free")
        rows_done = sem("rows_done")
        rows_kept = sem("rows_kept")
        den_ready = sem("den_ready")
        inv_den_ready = sem("inv_den_ready")
        out_ready = sem("out_ready")
        last_stored = sem("last_stored")
        rows_free = sem("rows_free")
        c_all_turned = sem("c_all_turned")
        c_turned_kept = sem("c_turned_kept")
        c_flat_stored = sem("c_flat_stored")
        c_row_loaded = sem("c_row_loaded")
        out_stored = [sem(f"out_stored{k}") for k in range(RB)]

        low_ready = sem("low_ready")
        low_counted = sem("low_counted")
        plain_known = sem("plain_known")
        d_col_ready = sem("d_col_ready")
        d_col_turned = sem("d_col_turned")
        d_row_kept = sem("d_row_kept")
        d_flat_stored = sem("d_flat_stored")
        d_row_loaded = sem("d_row_loaded")
        stores_complete = sem("stores_complete")
        adj_rows_loaded = sem("adj_rows_loaded")
        score_step = sem("score_step")
        scores_ready = sem("scores_ready")
        exp_ready = sem("exp_ready")
        weights_turned = sem("weights_turned")
        weights_kept = sem("weights_kept")
        block_done = sem("block_done")
        block_out_ready = sem("block_out_ready")
        block_stored = sem("block_stored")
        blocks_finished = sem("blocks_finished")

        d_row = c_row
        adj_rows = adj_sb[:].rearrange("p r w -> p (r w)")
        masks = adj_rows.bitcast(fp32)
        scores = p_sb[:].rearrange("p r w -> p (r w)")

        x_v = x.rearrange("(t p) f -> p t f", p=P)
        w_v = w.rearrange("(c p) k -> p c k", p=P)
        w_tv = w_t.rearrange("(c p) o -> p c o", p=P)
        out_v = out.rearrange("(t p) f -> p t f", p=P)
        edges = adj_t.bitcast(u32)

        def turned(part, t):
            ring, first = (hnt_hi, first_hi) if part == "hi" else (hnt_lo, first_lo)
            return first[:, :, t * P:(t + 1) * P] if t < RB else ring[:, :, t % R * P:(t % R + 1) * P]

        def in_chunks(bank):
            return ps[:, bank, 0:F].rearrange("p (c n) -> p c n", c=KC)

        block = ctx.enter_context(nc.Block())

        @block.sync
        def _(sp):
            sp.dma_start(w_nat[:], w_v).then_inc(w_nat_loaded, 16)
            for n, a in enumerate((a1, a2)):
                sp.dma_start(a_sb[:, :, n], a.rearrange("(c p) -> p c", p=P),
                             allow_slow_non_contiguous=True).then_inc(w_nat_loaded, 16)
            sp.dma_start(w_f[:, :, 0:F], w_tv).then_inc(w_t_loaded, 16)
            for m in range(T // XB):
                sp.dma_start(x_sb[:, m * XB:(m + 1) * XB, :], x_v[:, m * XB:(m + 1) * XB, :])\
                  .then_inc(x_loaded[m], 16)

            def load_edges(u, t, g):
                sp.dma_start(adj_sb[:, u % R, :], edges[bass.ds(t * P, P), bass.ds(g * WG, WG)])\
                  .then_inc(adj_loaded[u % R], 16)

            def load_tiles(g, q, first):
                for u in range(U):
                    if u >= R or not first:
                        sp.wait_ge(weights_ready, g * T + q * U + (u - R + 1))
                    load_edges(u, q * U + u, g)

            load_tiles(0, 0, True)
            sp.wait_ge(c_turned_kept, 1)
            sp.dma_start(c_flat, c_turned[:]).then_inc(c_flat_stored, 16)
            sp.wait_ge(c_flat_stored, 16)
            sp.dma_start(c_row[:, WG:N], c_flat.rearrange("t p -> (t p)")[WG:N].partition_broadcast(P))\
              .then_inc(c_row_loaded, 16)
            with sp.Fori(1, Q) as q:
                load_tiles(0, q, False)
            with sp.Fori(1, NG) as g:
                with sp.Fori(0, Q) as q:
                    load_tiles(g, q, False)

            for k in range(RB):
                sp.wait_ge(out_ready, (NG - 1) * RB + k + 1)
                sp.dma_start(out_v[:, (NG - 1) * RB + k, :], rows_sb[:, k, 0:F]).then_inc(last_stored, 16)
            sp.wait_ge(last_stored, 16 * RB)

            sp.wait_ge(plain_known, 1)
            needed = sp.value_load(plain_needed[0:1, 0:1], min_val=0, max_val=1)
            with sp.If(needed > 0):
                sp.sem_inc(stores_complete, 1)
                sp.wait_ge(d_row_kept, 1)
                sp.dma_start(c_flat, c_turned[:]).then_inc(d_flat_stored, 16)
                sp.wait_ge(d_flat_stored, 16)
                sp.dma_start(d_row[:], c_flat.rearrange("t p -> (t p)").partition_broadcast(P)).then_inc(d_row_loaded, 16)
                with sp.Fori(0, T) as b:
                    sp.dma_start(adj_rows, adj.bitcast(u32)[bass.ds(b * P, P), :]).then_inc(adj_rows_loaded, 16)
                    sp.wait_ge(block_out_ready, b + 1)
                    sp.dma_start(out_v[:, bass.ds(b, 1), :], rows_sb[:, 0:1, 0:F]).then_inc(block_stored, 16)
                    sp.wait_ge(block_stored, b * 16 + 16)
                    sp.sem_inc(blocks_finished, 1)

        @block.gpsimd
        def _(pool):
            nc.gpsimd.memset(ones[:], 1.0).then_inc(consts_ready, 1)
            nc.gpsimd.memset(eps_sb[:], EPS / HN_UP ** 2).then_inc(consts_ready, 1)
            pool.wait_ge(consts_ready, 2)
            nc.gpsimd.affine_select(out=ident[:], in_=ones[:], compare_op=ALU.is_equal, fill=0.0,
                                    base=0, pattern=[[-1, P]], channel_multiplier=1).then_inc(consts_ready, 1)

            nc.gpsimd.memset(up_row[:], 1 / H_DOWN).then_inc(consts_ready, 1)

            pool.sem_inc(rows_free, RB)
            nc.gpsimd.memset(v_sb[:, :, 0, F:FD], ONE_UP).then_inc(v_ones_ready, 1)

            for t in BY_GPSIMD:
                pool.wait_ge(shift_ready, t // XB + 1)
                if t >= RN:
                    pool.wait_ge(hn_turned, t - RN + 1)
                nc.gpsimd.tensor_scalar(hn_sb[:, t % RN, :], x_sb[:, t, :], moments[:, t, 0:1], rstd[:, t:t + 1],
                                        ALU.subtract, ALU.mult).then_inc(hn_gpsimd_ready, 1)

            with pool.Fori(0, T) as t:
                pool.wait_ge(v_hi_ready, t + 1)
                nc.gpsimd.tensor_tensor(v_sb[:, bass.ds(t, 1), 1, 0:F], h_sb[:, bass.ds(t, 1), 0:F],
                                        v_sb[:, bass.ds(t, 1), 0, 0:F], ALU.subtract).then_inc(v_lo_ready, 1)

            with pool.Fori(0, NG - 1) as g:
                for k in range(RB):
                    pool.wait_ge(out_ready, g * RB + (k + 1))
                    pool.dma_start(out_v[:, bass.ds(g * RB + k, 1), :], rows_sb[:, k:k + 1, 0:F])\
                        .then_inc(out_stored[k], 16)
                for k in range(RB):
                    pool.wait_ge(out_stored[k], g * 16 + 16)
                    pool.sem_inc(rows_free, 1)

        @block.scalar
        def _(act):
            def std_of(m):
                act.wait_ge(moments_ready, (m + 1) * XB)
                nc.scalar.activation(std[:, m * XB:(m + 1) * XB], moments[:, m * XB:(m + 1) * XB, 1], ACT.Sqrt,
                                     bias=eps_sb[:, 0:1], scale=HN_UP ** -2).then_inc(std_ready, 1)

            def keep_h(t):
                act.wait_ge(h_done, t + 1)
                nc.scalar.activation(h_sb[:, t, :], ps[:, bank_h + t % 2, 0:FW], ACT.Copy, scale=H_DOWN)\
                    .then_inc(h_kept, 1)

            def normalise(t):
                act.wait_ge(shift_ready, t // XB + 1)
                if t >= RN:
                    act.wait_ge(hn_turned, t - RN + 1)
                nc.scalar.activation(hn_sb[:, t % RN, :], x_sb[:, t, :], ACT.Identity, bias=shift[:, t:t + 1],
                                     scale=rstd[:, t:t + 1]).then_inc(hn_scalar_ready, 1)

            act.wait_ge(consts_ready, 2)
            nc.scalar.activation(warm[:], eps_sb[:], ACT.Sqrt)
            act.wait_ge(w_t_loaded, 16)
            nc.scalar.activation(squares[:], w_f[:, :, 0:F], ACT.Square, accum_out=sumsq[:, 0:1]).then_inc(sumsq_ready, 1)
            act.wait_ge(wa_done, 1)
            wa = ps[:, bank_w, 0:2 * KC].rearrange("p (c n) -> p c n", c=KC)
            nc.scalar.activation(squares_a[:], wa, ACT.Square, accum_out=sumsq[:, 1:2]).then_inc(sumsq_ready, 1)
            nc.scalar.activation(w_f[:, :, F:FW], wa, ACT.Copy).then_inc(wa_kept, 1)
            act.wait_ge(sumsq_summed, 1)
            nc.scalar.activation(norms[:], ps[:, bank_d, 0:2], ACT.Sqrt).then_inc(norms_ready, 1)
            act.wait_ge(wa_kept, 1)
            act.wait_ge(w_scale_ready, 1)
            for n, part in enumerate(W_PARTS):
                nc.scalar.activation(w_hi[:, :, part], w_f[:, :, part], ACT.Copy, scale=w_scale[:, n:n + 1])\
                    .then_inc(w_hi_ready, 1)
            std_of(0)
            normalise(1)
            for t in range(T):
                act.wait_ge(hn_turned, t + 1)
                if t >= R:
                    act.wait_ge(h_done, t - R + 1)
                nc.scalar.activation(turned("hi", t), in_chunks(banks_t[t % R]), ACT.Relu).then_inc(hnt_hi_ready, 1)
                if t % XB == 1 and t + 3 < T:
                    std_of(t // XB + 1)
                if t + 3 in BY_SCALAR:
                    normalise(t + 3)
                if t >= 1:
                    keep_h(t - 1)
            act.wait_ge(d_part_ready, 1)
            keep_h(T - 1)

            def values_hi(t):
                nc.scalar.activation(v_sb[:, bass.ds(t, 1), 0, 0:F], h_sb[:, bass.ds(t, 1), 0:F], ACT.Copy)\
                    .then_inc(v_hi_ready, 1)
            act.wait_ge(h_kept, T)
            values_hi(0)

            for m, (k0, k1) in enumerate(FIRST_PARTS):
                part = slice(k0 * P, k1 * P)
                act.wait_ge(t_row_ready, m + 1)
                nc.scalar.activation(c_row[:, part], t_row[:, part], ACT.Exp, scale=exp_scale[:, 4:5])\
                    .then_inc(c_exp_ready, 1)
                if m == 0:
                    act.wait_ge(exp_bias_ready, 1)
                    nc.scalar.activation(g_col[:], h_sb[:, :, F + 1], ACT.Exp, bias=exp_bias[:, 0:1],
                                         scale=exp_scale[:, 1:2]).then_inc(g_ready, 1)
                    nc.scalar.activation(p_scale[:], h_sb[:, :, F + 1], ACT.Exp, bias=exp_bias[:, 1:2],
                                         scale=exp_scale[:, 2:3]).then_inc(p_scale_ready, 1)
            act.wait_ge(p_scale_ready, 1)

            def split_hi(u, t, n):
                act.wait_ge(weights_ready, n + (u + 1))
                act.wait_ge(slot_free, n + (u + 1))
                nc.scalar.activation(p_hi[:, u % R, :], p_sb[:, u % R, :], ACT.Copy, scale=p_scale[:, bass.ds(t, 1)])\
                    .then_inc(p_hi_ready, 1)

            def split_first_parts():
                for m, (k0, k1) in enumerate(FIRST_PARTS):
                    part = slice(k0 * P, k1 * P)
                    last = m == len(FIRST_PARTS) - 1
                    if last:
                        act.wait_ge(weights_ready, 1)
                    else:
                        act.wait_ge(part_weights_ready, m + 1)
                    nc.scalar.activation(p_hi[:, 0, part], p_sb[:, 0, part], ACT.Copy, scale=p_scale[:, 0:1])\
                        .then_inc(p_hi_ready if last else part_hi_ready, 1)
                    if m == 1:
                        act.wait_ge(t_col_ready, 1)
                        nc.scalar.activation(c_col[:], t_col[:], ACT.Exp, scale=exp_scale[:, 0:1]).then_inc(c_col_ready, 1)
                act.wait_ge(c_all_turned, 1)
                nc.scalar.activation(c_turned[:], ps[0:T, RB - 1, turned_c], ACT.Copy).then_inc(c_turned_kept, 1)

            def keep_rows(g):
                for k in range(RB):
                    act.wait_ge(rows_free, g * RB + (k + 1))
                    act.wait_ge(rows_done, g * RB + (k + 1))
                    nc.scalar.activation(rows_sb[:, k, :], ps[:, k, 0:FD], ACT.Copy).then_inc(rows_kept, 1)
                act.sem_inc(slot_free, 1)

            def tiles_group0(q, first):
                for u in range(U):
                    t = q * U + u
                    if first and u == 0:
                        split_first_parts()
                    else:
                        values_hi(t)
                        split_hi(u, t, q * U)
            tiles_group0(0, True)
            with act.Fori(1, Q) as q:
                tiles_group0(q, False)
            with act.Fori(1, NG) as g:
                for u in range(U):
                    if u == AHEAD:
                        keep_rows(g - 1)
                    split_hi(u, u, g * T)
                with act.Fori(1, Q) as q:
                    for u in range(U):
                        split_hi(u, q * U + u, g * T + q * U)

            act.wait_ge(plain_known, 1)
            needed = act.value_load(plain_needed[0:1, 0:1], min_val=0, max_val=1)
            with act.If(needed > 0):
                act.wait_ge(d_col_turned, 1)
                nc.scalar.activation(c_turned[:], ps[0:T, 0, 0:P], ACT.Copy).then_inc(d_row_kept, 1)
                with act.Fori(0, T) as b:
                    act.wait_ge(scores_ready, b + 1)
                    nc.scalar.activation(scores, scores, ACT.Exp, bias=row_max[:, 1:2], accum_out=row_sum[:])\
                        .then_inc(exp_ready, 1)

        @block.vector
        def _(dve):
            steps = [0]

            def link(instruction):
                steps[0] += 1
                instruction.then_inc(dve_step, 1)
                dve.wait_ge(dve_step, steps[0])

            def stats_of(t):
                if t % XB == 0:
                    dve.wait_ge(x_loaded[t // XB], 16)
                nc.vector.bn_stats(stats[:, t, :], x_sb[:, t, :]).then_inc(stats_ready, 1)

            def gather(t):
                dve.wait_ge(stats_ready, t + 1)
                nc.vector.bn_aggr(moments[:, t, :], stats[:, t, :]).then_inc(moments_ready, 1)

            def rstd_of(m):
                dve.wait_ge(std_ready, m + 1)
                batch = slice(m * XB, (m + 1) * XB)
                nc.vector.reciprocal(rstd[:, batch], std[:, batch]).then_inc(rstd_ready, 1)
                dve.wait_ge(rstd_ready, m + 1)
                nc.vector.scalar_tensor_tensor(out=shift[:, batch], in0=moments[:, batch, 0], scalar=-1.0,
                                               in1=rstd[:, batch], op0=ALU.mult, op1=ALU.mult).then_inc(shift_ready, 1)

            def split_hn_lo(t):
                dve.wait_ge(hnt_hi_ready, t + 1)
                nc.vector.scalar_tensor_tensor(out=turned("lo", t), in0=in_chunks(banks_t[t % R]), scalar=0.0,
                                               in1=turned("hi", t), op0=ALU.max, op1=ALU.subtract)\
                    .then_inc(hnt_lo_ready, 1)

            def normalise(t):
                if t >= RN:
                    dve.wait_ge(hn_turned, t - RN + 1)
                nc.vector.tensor_scalar(hn_sb[:, t % RN, :], x_sb[:, t, :], moments[:, t, 0:1], rstd[:, t:t + 1],
                                        ALU.subtract, ALU.mult).then_inc(hn_vector_ready, 1)

            stats_of(0)
            stats_of(1)
            gather(0)
            gather(1)
            dve.wait_ge(norms_ready, 1)
            link(nc.vector.tensor_scalar(norms[:], norms[:], 1e-15, None, ALU.max))
            link(nc.vector.reciprocal(inv_norms[:], norms[:]))
            nc.vector.tensor_scalar(w_scale[:], inv_norms[:], W_UP, None, ALU.mult).then_inc(w_scale_ready, 1)
            stats_of(2)
            stats_of(3)
            gather(2)
            gather(3)
            dve.wait_ge(w_scale_ready, 1)
            for n, part in enumerate(W_PARTS):
                dve.wait_ge(w_hi_ready, n + 1)
                nc.vector.scalar_tensor_tensor(out=w_lo[:, :, part], in0=w_f[:, :, part], scalar=w_scale[:, n:n + 1],
                                               in1=w_hi[:, :, part], op0=ALU.mult, op1=ALU.subtract).then_inc(w_lo_ready, 1)
            rstd_of(0)
            normalise(0)
            normalise(2)
            stats_of(4)
            stats_of(5)
            gather(4)
            stats_of(6)
            gather(5)

            stats_tiles = {0: (7,), 1: (8,), 2: (9, 10)}
            for t in range(T):
                ahead = stats_tiles.get(t, (t + 8,))
                split_hn_lo(t)
                if ahead[0] <= T:
                    gather(ahead[0] - 1)
                if t % XB == 1 and t + 3 < T:
                    rstd_of(t // XB + 1)
                if t + 3 in BY_VECTOR:
                    normalise(t + 3)
                for n in ahead:
                    if n > ahead[0]:
                        gather(n - 1)
                    if n < T:
                        stats_of(n)
                if t == T - 6:
                    nc.vector.tensor_copy(w1_hi[:], w_hi[:, :, F:F + 1].to_broadcast([P, KC, P])).then_inc(w1_ready, 1)
                    dve.wait_ge(w_lo_ready, 2)
                    nc.vector.tensor_copy(w1_lo[:], w_lo[:, :, F:F + 1].to_broadcast([P, KC, P])).then_inc(w1_ready, 1)
                    for n, factor in enumerate((-0.8, 0.8, 0.2, -0.2, -0.8 * H_DOWN)):
                        last = nc.vector.tensor_scalar(exp_scale[:, n:n + 1], norms[:, 1:2], factor / H_UP, None, ALU.mult)
                    link(last)
                    link(nc.vector.tensor_scalar(den_scale[:], inv_norms[:, 0:1], H_UP / ONE_UP, None, ALU.mult))
                    nc.vector.tensor_scalar(den_low[:], inv_norms[:, 0:1], DEN_LOW * H_UP / ONE_UP, None, ALU.mult)

            dve.wait_ge(h_kept, T - 1)
            link(nc.vector.tensor_reduce(d_most[:], h_sb[:, 0:T - 1, F + 1], AX.X, ALU.max))
            dve.wait_ge(h_done, T)
            nc.vector.scalar_tensor_tensor(out=d_part[:], in0=ps[:, bank_h + (T - 1) % 2, F + 1:F + 2], scalar=H_DOWN,
                                           in1=d_most[:], op0=ALU.mult, op1=ALU.max).then_inc(d_part_ready, 1)
            dve.wait_ge(d_turned, 1)
            nc.vector.tensor_reduce(d_one[:], ps[0:1, bank_d, 0:P], AX.X, ALU.max).then_inc(d_one_ready, 1)
            dve.wait_ge(d_spread, 1)

            def t_row_part(k0, k1):
                dve.wait_ge(s_spread, k0 // CT + 1)
                bank, column = bank_s + k0 // CT, k0 % CT * P
                nc.vector.tensor_scalar(t_row[:, k0 * P:k1 * P], ps[:, bank, column:column + (k1 - k0) * P],
                                        ps[:, bank_d, P + 1:P + 2], 0.0, ALU.add, ALU.max).then_inc(t_row_ready, 1)

            t_row_part(*FIRST_PARTS[0])
            nc.vector.tensor_scalar(exp_bias[:, 1:2], exp_scale[:, 3:4], ps[:, bank_d, P:P + 1], math.log(P_UP),
                                    ALU.mult, ALU.add)
            nc.vector.tensor_scalar(exp_bias[:, 0:1], exp_scale[:, 0:1], ps[:, bank_d, P:P + 1], None, ALU.mult)\
                .then_inc(exp_bias_ready, 1)
            for k0, k1 in FIRST_PARTS[1:]:
                t_row_part(k0, k1)
            dve.wait_ge(h_kept, T)
            nc.vector.tensor_scalar(t_col[:], h_sb[:, :, F], ps[:, bank_d, P:P + 1], 0.0, ALU.add, ALU.max)\
                .then_inc(t_col_ready, 1)

            for m, (k0, k1) in enumerate(FIRST_PARTS):
                part = slice(k0 * P, k1 * P)
                dve.wait_ge(c_exp_ready, m + 1)
                if m == 0:
                    dve.wait_ge(g_ready, 1)
                    dve.wait_ge(adj_loaded[0], 16)
                nc.vector.scalar_tensor_tensor(out=p_sb[:, 0, part], in0=c_row[:, part], scalar=g_col[:, 0:1],
                                               in1=adj_sb[:, 0, part], op0=ALU.max, op1=ALU.min)\
                    .then_inc(weights_ready if m == len(FIRST_PARTS) - 1 else part_weights_ready, 1)
            dve.wait_ge(p_scale_ready, 1)

            def edge_weights(u, t, loads, g):
                dve.wait_ge(adj_loaded[u % R], loads)
                nc.vector.scalar_tensor_tensor(out=p_sb[:, u % R, :], in0=c_row[:, bass.ds(g * WG, WG)],
                                               scalar=g_col[:, bass.ds(t, 1)], in1=adj_sb[:, u % R, :],
                                               op0=ALU.max, op1=ALU.min).then_inc(weights_ready, 1)

            def split_lo(u, t, n):
                dve.wait_ge(p_hi_ready, n + (u + 1))
                nc.vector.scalar_tensor_tensor(out=p_lo[:, u % R, :], in0=p_sb[:, u % R, :], scalar=p_scale[:, bass.ds(t, 1)],
                                               in1=p_hi[:, u % R, :], op0=ALU.mult, op1=ALU.subtract)\
                    .then_inc(p_lo_ready, 1)

            def inverses(g, half):
                a = half * HALF
                dve.wait_ge(rows_kept, g * RB + (a + HALF))
                nc.vector.tensor_scalar(den[:, bass.ds(g * RB + a, HALF)], rows_sb[:, a:a + HALF, F], den_scale[:, 0:1],
                                        DEN_TINY, ALU.mult, ALU.max).then_inc(den_ready, 1)
                dve.wait_ge(den_ready, g * 2 + (half + 1))
                nc.vector.reciprocal(inv_den[:, bass.ds(g * RB + a, HALF)], den[:, bass.ds(g * RB + a, HALF)])\
                    .then_inc(inv_den_ready, 1)
                dve.wait_ge(inv_den_ready, g * 2 + (half + 1))

            def rows_out(g, k):
                b = g * RB + k
                nc.vector.scalar_tensor_tensor(out=rows_sb[:, k:k + 1, 0:F], in0=rows_sb[:, k:k + 1, 0:F],
                                               scalar=inv_den[:, bass.ds(b, 1)], in1=x_sb[:, bass.ds(b, 1), :],
                                               op0=ALU.mult, op1=ALU.add).then_inc(out_ready, 1)

            def tiles_group0(q, first):
                for u in range(U):
                    if u > 0 or not first:
                        edge_weights(u, q * U + u, q * 32 + 16 * (u // R + 1), 0)
                    if u > 0 or not first:
                        split_lo(u - 1, q * U + (u - 1), q * U)

            def tiles(g, q, first):
                for u in range(U):
                    edge_weights(u, q * U + u, g * (32 * Q) + q * 32 + 16 * (u // R + 1), g)
                    if u > 0 or not first:
                        split_lo(u - 1, q * U + (u - 1), g * T + q * U)
                    if first and AHEAD < u <= AHEAD + RB // 2:
                        if (u - AHEAD - 1) % 2 == 0:
                            inverses(g - 1, (u - AHEAD - 1) // 2)
                        for k in range(2 * (u - AHEAD - 1), 2 * (u - AHEAD)):
                            rows_out(g - 1, k)

            tiles_group0(0, True)
            with dve.Fori(1, Q) as q:
                tiles_group0(q, False)
            split_lo(U - 1, T - 1, T - U)
            dve.wait_ge(c_row_loaded, 16)
            with dve.Fori(1, NG) as g:
                tiles(g, 0, True)
                with dve.Fori(1, Q) as q:
                    tiles(g, q, False)
                split_lo(U - 1, T - 1, g * T + (T - U))
            for k in range(0, RB, 2):
                b = (NG - 1) * RB + k
                dve.wait_ge(rows_done, b + 2)
                link(nc.vector.tensor_scalar(den[:, b:b + 2], ps[:, k:k + 2, F], den_scale[:, 0:1], DEN_TINY,
                                             ALU.mult, ALU.max))
                link(nc.vector.reciprocal(inv_den[:, b:b + 2], den[:, b:b + 2]))
                if k == 0:
                    dve.wait_ge(rows_free, (NG - 1) * RB + RB)
                for n in (0, 1):
                    nc.vector.scalar_tensor_tensor(out=rows_sb[:, k + n, 0:F], in0=ps[:, k + n, 0:F],
                                                   scalar=inv_den[:, b + n:b + n + 1], in1=x_sb[:, b + n, :],
                                                   op0=ALU.mult, op1=ALU.add).then_inc(out_ready, 1)

            link(nc.vector.tensor_reduce(den_least[:], den[:], AX.X, ALU.min))
            nc.vector.tensor_tensor(den_is_low[:], den_least[:], den_low[:], ALU.is_lt).then_inc(low_ready, 1)
            dve.wait_ge(low_counted, 1)
            nc.vector.tensor_scalar(plain_needed[:], ps[0:1, 0, 0:1], 1.0, None, ALU.min).then_inc(plain_known, 1)
            dve.wait_ge(plain_known, 1)
            needed = dve.value_load(plain_needed[0:1, 0:1], min_val=0, max_val=1)
            with dve.If(needed > 0):
                link(nc.vector.tensor_scalar(unit[:], norms[:, 1:2], 1.0 / H_UP, None, ALU.mult))
                nc.vector.tensor_scalar(d_col[:], h_sb[:, :, F + 1], unit[:, 0:1], None, ALU.mult).then_inc(d_col_ready, 1)
                link(nc.vector.tensor_scalar(s_col[:], h_sb[:, :, F], unit[:, 0:1], None, ALU.mult))
                dve.wait_ge(stores_complete, 1)
                dve.wait_ge(d_row_loaded, 16)
                SCORE_STEPS = 8
                with dve.Fori(0, T) as b:
                    def ordered(step, instruction):
                        instruction.then_inc(score_step, 1)
                        dve.wait_ge(score_step, b * SCORE_STEPS + (step + 1))

                    ordered(0, nc.vector.tensor_scalar(scores, d_row[:], s_col[:, bass.ds(b, 1)], None, ALU.add))
                    ordered(1, nc.vector.scalar_tensor_tensor(out=scores, in0=scores, scalar=SLOPE, in1=scores,
                                                              op0=ALU.mult, op1=ALU.max))
                    dve.wait_ge(adj_rows_loaded, b * 16 + 16)
                    ordered(2, nc.vector.scalar_tensor_tensor(out=scores, in0=adj_rows, scalar=0.0, in1=scores,
                                                              op0=ALU.not_equal, op1=ALU.mult))
                    ordered(3, nc.vector.tensor_scalar(masks, adj_rows, 0.0, NEG_INF, ALU.is_equal, ALU.mult))
                    ordered(4, nc.vector.tensor_tensor(scores, scores, masks, ALU.add))
                    ordered(5, nc.vector.tensor_reduce(row_max[:, 0:1], scores, AX.X, ALU.max))
                    nc.vector.tensor_scalar(row_max[:, 1:2], row_max[:, 0:1], -1.0, None, ALU.mult)\
                        .then_inc(scores_ready, 1)
                    for n in range(T // GC):
                        dve.wait_ge(weights_turned, b * (T // GC) + (n + 1))
                        half = 2 + 2 * (n % 2)
                        nc.vector.tensor_copy(rows_sb[:, half:half + 2, 0:F],
                                              ps[:, 1 + n % 2, :].rearrange("p (a f) -> p a f", a=2))\
                            .then_inc(weights_kept, 1)
                    dve.wait_ge(exp_ready, b + 1)
                    ordered(6, nc.vector.tensor_scalar(row_inv[:, 0:1], row_sum[:], den_scale[:, 0:1], ONE_UP,
                                                       ALU.mult, ALU.mult))
                    ordered(7, nc.vector.reciprocal(row_inv[:, 1:2], row_inv[:, 0:1]))
                    dve.wait_ge(block_done, b + 1)
                    nc.vector.scalar_tensor_tensor(out=rows_sb[:, 0:1, 0:F], in0=ps[:, 0:1, 0:F], scalar=row_inv[:, 1:2],
                                                   in1=x_sb[:, bass.ds(b, 1), :], op0=ALU.mult, op1=ALU.add)\
                        .then_inc(block_out_ready, 1)

        @block.tensor
        def _(pe):
            pe.sem_inc(slot_free, R)

            def keep_busy(bank, count):
                for _ in range(count):
                    nc.tensor.matmul(ps[:, bank, 0:P], ones[:], ones[:], start=True, stop=True)

            pe.wait_ge(consts_ready, 1)
            keep_busy(banks_t[0], BUSY_START)

            pe.wait_ge(w_nat_loaded, 48)
            for c in range(KC):
                for o in range(KC):
                    last = nc.tensor.matmul(ps[:, bank_w, 2 * c:2 * c + 2], w_nat[:, o, c * P:(c + 1) * P], a_sb[:, o, :],
                                            start=(o == 0), stop=(o == KC - 1))
            last.then_inc(wa_done, 1)
            pe.wait_ge(sumsq_ready, 2)
            nc.tensor.matmul(ps[:, bank_d, 0:2], ones[:], sumsq[:], start=True, stop=True).then_inc(sumsq_summed, 1)
            keep_busy(banks_t[1], BUSY_SPLIT)

            def turn(t):
                for tiles_of, ready in ((BY_VECTOR, hn_vector_ready), (BY_SCALAR, hn_scalar_ready),
                                        (BY_GPSIMD, hn_gpsimd_ready)):
                    if t in tiles_of:
                        pe.wait_ge(ready, tiles_of.index(t) + 1)
                if t >= R:
                    pe.wait_ge(hnt_lo_ready, t - R + 1)
                for c in range(KC):
                    last = nc.tensor.transpose(ps[:, banks_t[t % R], c * P:(c + 1) * P],
                                               hn_sb[:, t % RN, c * P:(c + 1) * P], ident[:])
                last.then_inc(hn_turned, 1)

            def project(t):
                pe.wait_ge(hnt_hi_ready, t + 1)
                if t >= 2:
                    pe.wait_ge(h_kept, t - 1)
                o = ps[:, bank_h + t % 2, 0:FW]
                for c in range(KC):
                    a = turned("hi", t)[:, c, :]
                    nc.tensor.matmul(o, a, w_hi[:, c, :], start=(c == 0), stop=False)
                    nc.tensor.matmul(o, a, w_lo[:, c, :], start=False, stop=False)
                pe.wait_ge(hnt_lo_ready, t + 1)
                for c in range(KC):
                    last = nc.tensor.matmul(o, turned("lo", t)[:, c, :], w_hi[:, c, :],
                                            start=False, stop=(c == KC - 1))
                last.then_inc(h_done, 1)

            def spread_s(m, c):
                part = slice(m * CW, (m + 1) * CW)
                last_chunk = c == KC - 1
                nc.tensor.matmul(ps[:, bank_s + m, :], w1_hi[:, c, :], first_hi[:, c, part], start=(c == 0), stop=False)
                nc.tensor.matmul(ps[:, bank_s + m, :], w1_lo[:, c, :], first_hi[:, c, part], start=False, stop=False)
                last = nc.tensor.matmul(ps[:, bank_s + m, :], w1_hi[:, c, :], first_lo[:, c, part],
                                        start=False, stop=last_chunk)
                if last_chunk:
                    last.then_inc(s_spread, 1)

            pe.wait_ge(consts_ready, 4)
            turn(0)
            turn(1)
            pe.wait_ge(w_lo_ready, 2)
            for t in range(T):
                if t + 2 < T:
                    turn(t + 2)
                project(t)

            pe.wait_ge(w1_ready, 2)
            spread_s(0, 0)
            pe.wait_ge(d_part_ready, 1)
            nc.tensor.transpose(ps[0:1, bank_d, 0:P], d_part[:], ident[:]).then_inc(d_turned, 1)
            spread_s(0, 1)
            pe.wait_ge(d_one_ready, 1)
            nc.tensor.matmul(ps[:, bank_d, P:P + 1], ones[0:1, :], d_one[:], start=True, stop=True)
            nc.tensor.matmul(ps[:, bank_d, P + 1:P + 2], up_row[:], d_one[:], start=True, stop=True).then_inc(d_spread, 1)
            spread_s(1, 0)
            spread_s(1, 1)
            keep_busy(banks_t[1], BUSY_C)

            def product(u, t, k, part, v, start, stop):
                width = F if v else FD
                return nc.tensor.matmul(ps[:, k, 0:width], part[:, u % R, k * P:(k + 1) * P],
                                        v_sb[:, bass.ds(t, 1), v, 0:width],
                                        start=start, stop=stop, skip_group_check=True)

            def sums(u, t, n, g, first):
                if not (first and g is None):
                    pe.wait_ge(p_hi_ready, n + (u + 1))
                for k in range(RB):
                    if first and g is None:
                        for m, (k0, _) in enumerate(FIRST_PARTS[:-1]):
                            if k == k0:
                                pe.wait_ge(part_hi_ready, m + 1)
                        if k == FIRST_PARTS[-1][0]:
                            pe.wait_ge(c_col_ready, 1)
                            nc.tensor.transpose(ps[0:T, RB - 1, turned_c], c_col[:], ident[:]).then_inc(c_all_turned, 1)
                            pe.wait_ge(p_hi_ready, 1)
                    if first and g is None and k == RB - 1:
                        pe.wait_ge(c_turned_kept, 1)
                    if first and g is not None:
                        pe.wait_ge(rows_kept, (g - 1) * RB + (k + 1))
                    product(u, t, k, p_hi, 0, first, False)
                    product(u, t, k, p_hi, 1, False, False)
                pe.wait_ge(p_lo_ready, n + (u + 1))
                for k in range(RB):
                    done = product(u, t, k, p_lo, 0, False, False)
                done.then_inc(slot_free, 1)

            def last_sums(t, n):
                pe.wait_ge(p_lo_ready, n + U)
                for k in range(RB):
                    for u in (U - 2, U - 1):
                        product(u, t + u, k, p_hi, 0, False, False)
                        product(u, t + u, k, p_hi, 1, False, False)
                        done = product(u, t + u, k, p_lo, 0, False, u == U - 1)
                        if u == U - 2 and k == RB - 1:
                            done.then_inc(slot_free, 1)
                    done.then_inc(rows_done, 1)

            def tiles(g, q, first, last):
                n = q * U if g is None else g * T + q * U
                for u in range(U - 2 if last else U):
                    if g is None:
                        pe.wait_ge(v_lo_ready, n + (u + 1))
                    sums(u, q * U + u, n, g, first and u == 0)
                if last:
                    if g is None:
                        pe.wait_ge(v_lo_ready, T)
                    last_sums(q * U, n)

            def group(g):
                tiles(g, 0, True, False)
                with pe.Fori(1, Q - 1) as q:
                    tiles(g, q, False, False)
                tiles(g, Q - 1, False, True)

            pe.wait_ge(v_ones_ready, 1)
            group(None)
            with pe.Fori(1, NG) as g:
                group(g)

            pe.wait_ge(low_ready, 1)
            nc.tensor.matmul(ps[0:1, 0, 0:1], den_is_low[:], ones[:, 0:1], start=True, stop=True).then_inc(low_counted, 1)
            pe.wait_ge(plain_known, 1)
            needed = pe.value_load(plain_needed[0:1, 0:1], min_val=0, max_val=1)
            with pe.If(needed > 0):
                pe.wait_ge(d_col_ready, 1)
                nc.tensor.transpose(ps[0:T, 0, 0:P], d_col[:], ident[:]).then_inc(d_col_turned, 1)
                with pe.Fori(0, T) as b:
                    def turn_weights(n):
                        for c in range(GC):
                            j = (n * GC + c) * P
                            last = nc.tensor.transpose(ps[:, 1 + n % 2, c * P:(c + 1) * P], scores[:, j:j + P], ident[:])
                        last.then_inc(weights_turned, 1)

                    pe.wait_ge(exp_ready, b + 1)
                    turn_weights(0)
                    for n in range(T // GC):
                        if n + 1 < T // GC:
                            turn_weights(n + 1)
                        pe.wait_ge(weights_kept, b * (T // GC) + (n + 1))
                        for c in range(GC):
                            half = 2 + 2 * (n % 2) + c // 2
                            last = nc.tensor.matmul(ps[:, 0, 0:F], rows_sb[:, half, (c % 2) * P:(c % 2 + 1) * P],
                                                    h_sb[:, n * GC + c, 0:F], start=(n + c == 0),
                                                    stop=(n * GC + c == T - 1))
                    last.then_inc(block_done, 1)


def kernel(x, adj, L0_gnn_W, L0_gnn_a1, L0_gnn_a2):
    import numpy as np
    import concourse.bacc as bacc
    from concourse.bass_utils import run_bass_kernel_spmd as run

    w = np.asarray(L0_gnn_W)
    arrays = {
        "x": np.ascontiguousarray(x),
        "adj": np.ascontiguousarray(adj),
        "adj_t": np.ascontiguousarray(np.asarray(adj).T),
        "w": np.ascontiguousarray(w),
        "w_t": np.ascontiguousarray(w.T),
        "a1": np.ascontiguousarray(L0_gnn_a1),
        "a2": np.ascontiguousarray(L0_gnn_a2),
    }
    nc = bacc.Bacc("TRN2", target_bir_lowering=False, num_devices=1)
    args = [nc.dram_tensor(name, a.shape, mybir.dt.from_np(a.dtype), kind="ExternalInput").ap()
            for name, a in arrays.items()]
    out = nc.dram_tensor("out", arrays["x"].shape, mybir.dt.float32, kind="ExternalOutput").ap()
    gat_layer(nc, *args, out)
    return run(nc, [arrays], core_ids=[0]).results[0]["out"]
```
